# Optimizing a Trainium2 kernel written in Bass

```python
import numpy as np
import jax
import jax.numpy as jnp

def _softmax(x, axis=-1):
    return jax.nn.softmax(x, axis=axis)

def _gelu(x):
    return jax.nn.gelu(x, approximate=True)

def _silu(x):
    return jax.nn.silu(x)

def _sigmoid(x):
    return jax.nn.sigmoid(x)

def _layernorm(x, axis=-1, eps=1e-05):
    m = jnp.mean(x, axis=axis, keepdims=True)
    v = jnp.var(x, axis=axis, keepdims=True)
    return (x - m) / jnp.sqrt(v + eps)

def _scatter_add(tgt, idx, src, axis=0):
    return tgt.at[idx].add(src)

def _segment_sum(src, seg, n):
    return jax.ops.segment_sum(src, seg, n)
kernel_name = 'mk_seq_postln_d1_jaxref_r4_79ec0b'

def setup_inputs(seed: int=0):
    np.random.seed(seed)
    _w = jnp.asarray

    def _L0_attn_setup():
        import jax, jax.numpy as jnp
        import numpy as np
        H = 16
        DK = 128
        DV = 128
        M = 64
        EPS = 1e-05
        CLAMP = 32.0
        ROPE_BASE = 10000.0

        def _rope(x, cos, sin):
            x1, x2 = jnp.split(x, 2, axis=-1)
            return jnp.concatenate([x1 * cos - x2 * sin, x2 * cos + x1 * sin], axis=-1)
        key = jax.random.key(seed)
        ks = jax.random.split(key, 9)
        B, T, D = (1, 512, 512)
        sc = 0.02
        return {'hidden_states': jax.random.normal(ks[0], (B, T, D), jnp.float32), 'Wq': jax.random.normal(ks[1], (H * DK, D), jnp.float32) * sc, 'Wk': jax.random.normal(ks[2], (H * DK, D), jnp.float32) * sc, 'Wv': jax.random.normal(ks[3], (H * DV, D), jnp.float32) * sc, 'Wg': jax.random.normal(ks[4], (H * DV, D), jnp.float32) * sc, 'Wo': jax.random.normal(ks[5], (D, H * DV), jnp.float32) * sc, 'Ws1': jax.random.normal(ks[6], (16, D), jnp.float32) * sc, 'Ws2': jax.random.normal(ks[7], (H * M, 16), jnp.float32) * sc, 'bs2': jnp.zeros((H * M,), jnp.float32), 'g_norm_weight': jnp.ones((DV,), jnp.float32)}
    _L0_attn_in = _L0_attn_setup()

    def _L0_ffn_setup():
        import jax, jax.numpy as jnp
        import numpy as np
        key = jax.random.key(seed)
        k1, k2, k3, k4 = jax.random.split(key, 4)
        B, S, D_IN, D_OUT = (4, 1024, 512, 512)
        x = jax.random.normal(k1, (B, S, D_IN), dtype=jnp.float32)
        weight = jax.random.normal(k2, (D_OUT, D_IN), dtype=jnp.float32) * 0.02
        scale_weight = jax.random.uniform(k3, (D_OUT,), dtype=jnp.float32, minval=0.5, maxval=1.5)
        bias = jax.random.normal(k4, (D_OUT,), dtype=jnp.float32) * 0.02
        return {'x': x, 'weight': weight, 'scale_weight': scale_weight, 'bias': bias}
    _L0_ffn_in = _L0_ffn_setup()
    _d = {'L0_attn_hidden_states': _L0_attn_in['hidden_states'], 'L0_attn_Wq': _L0_attn_in['Wq'], 'L0_attn_Wk': _L0_attn_in['Wk'], 'L0_attn_Wv': _L0_attn_in['Wv'], 'L0_attn_Wg': _L0_attn_in['Wg'], 'L0_attn_Wo': _L0_attn_in['Wo'], 'L0_attn_Ws1': _L0_attn_in['Ws1'], 'L0_attn_Ws2': _L0_attn_in['Ws2'], 'L0_attn_bs2': _L0_attn_in['bs2'], 'L0_attn_g_norm_weight': _L0_attn_in['g_norm_weight'], 'L0_ffn_weight': _L0_ffn_in['weight'], 'L0_ffn_scale_weight': _L0_ffn_in['scale_weight'], 'L0_ffn_bias': _L0_ffn_in['bias']}
    _x0 = _d['L0_attn_hidden_states']
    _d['L0_attn_hidden_states'] = jax.random.normal(jax.random.fold_in(jax.random.key(seed), 1), (4, 512, 512), dtype=_x0.dtype)
    del _x0
    return _d

def reference(L0_attn_hidden_states, L0_attn_Wq, L0_attn_Wk, L0_attn_Wv, L0_attn_Wg, L0_attn_Wo, L0_attn_Ws1, L0_attn_Ws2, L0_attn_bs2, L0_attn_g_norm_weight, L0_ffn_weight, L0_ffn_scale_weight, L0_ffn_bias):

    def _L0_attn_ref(hidden_states, Wq, Wk, Wv, Wg, Wo, Ws1, Ws2, bs2, g_norm_weight):
        import jax, jax.numpy as jnp
        import numpy as np
        H = 16
        DK = 128
        DV = 128
        M = 64
        EPS = 1e-05
        CLAMP = 32.0
        ROPE_BASE = 10000.0

        def _rope(x, cos, sin):
            x1, x2 = jnp.split(x, 2, axis=-1)
            return jnp.concatenate([x1 * cos - x2 * sin, x2 * cos + x1 * sin], axis=-1)
        B, T, D = hidden_states.shape
        hs = hidden_states
        q = (hs @ Wq.T).reshape(B, T, H, DK)
        k = (hs @ Wk.T).reshape(B, T, H, DK)
        pos = jnp.arange(T, dtype=jnp.float32)
        inv_freq = 1.0 / ROPE_BASE ** (jnp.arange(0, DK, 2, dtype=jnp.float32) / DK)
        ang = pos[:, None] * inv_freq[None, :]
        cos = jnp.cos(ang)[None, :, None, :]
        sin = jnp.sin(ang)[None, :, None, :]
        q = _rope(q, cos, sin).transpose(0, 2, 1, 3)
        k = _rope(k, cos, sin).transpose(0, 2, 1, 3)
        v = (hs @ Wv.T).reshape(B, T, H, DV).transpose(0, 2, 1, 3)
        s = hs @ Ws1.T @ Ws2.T + bs2
        s = jnp.clip(s, -CLAMP, CLAMP).reshape(B, T, H, M).transpose(0, 2, 1, 3)
        z = jax.lax.cumlogsumexp(s, axis=2)
        es = jnp.exp(s)
        enz = jnp.exp(-z)
        scale = DK ** (-0.5)
        mask = jnp.tril(jnp.ones((T, T), dtype=bool))
        A = jnp.einsum('bhtd,bhjd->bhtj', q, k) * scale
        A = jnp.where(mask, A, 0.0)
        ok = enz * jnp.einsum('bhtj,bhjm->bhtm', A, es)
        qv = jax.nn.softmax(ok, axis=-1)
        W2 = jnp.einsum('bhtm,bhjm->bhtj', qv * enz, es)
        W2 = jnp.where(mask, W2, 0.0)
        o = jnp.einsum('bhtj,bhjd->bhtd', W2, v)
        o = o.transpose(0, 2, 1, 3)
        g = (hs @ Wg.T).reshape(B, T, H, DV)
        o_n = o * jax.lax.rsqrt(jnp.mean(o * o, axis=-1, keepdims=True) + EPS) * g_norm_weight
        o_g = o_n * (g * jax.nn.sigmoid(g))
        return o_g.reshape(B, T, H * DV) @ Wo.T

    def _L0_ffn_ref(x, weight, scale_weight, bias):
        import jax, jax.numpy as jnp
        import numpy as np
        w = weight * scale_weight[:, None]
        out = jnp.einsum('bsi,oi->bso', x, w) + bias
        return out
    x = L0_attn_hidden_states
    x = _layernorm(x + _L0_attn_ref(x, L0_attn_Wq, L0_attn_Wk, L0_attn_Wv, L0_attn_Wg, L0_attn_Wo, L0_attn_Ws1, L0_attn_Ws2, L0_attn_bs2, L0_attn_g_norm_weight), axis=-1)
    x = _layernorm(x + _L0_ffn_ref(x, L0_ffn_weight, L0_ffn_scale_weight, L0_ffn_bias), axis=-1)
    return x

_drawn_inputs = setup_inputs


def setup_inputs(seed=0):
    import zlib

    import numpy as np

    out = dict(_drawn_inputs(seed))
    spreads = {'L0_attn_bs2': (0.0, 0.8), 'L0_attn_g_norm_weight': (1.0, 0.2)}
    factors = {'L0_attn_Wq': 8.0,
     'L0_attn_Wk': 8.0,
     'L0_attn_Ws1': 8.0,
     'L0_attn_Ws2': 8.0,
     'L0_ffn_bias': 3.39}
    for name, (base, spread) in spreads.items():
        noise = np.random.default_rng([zlib.crc32(name.encode()), seed]).standard_normal(out[name].shape)
        drawn = base * np.exp(spread * noise) if base else spread * noise
        out[name] = jnp.asarray(drawn.astype(out[name].dtype))
    for name, factor in factors.items():
        out[name] = (out[name] * factor).astype(out[name].dtype)
    return out
```

```python
from contextlib import ExitStack

import concourse.bass as bass
from concourse import mybir

P = 128
BATCH, T, D = 4, 512, 512
HEADS, DK, DV, M = 16, 128, 128, 64
RANK = 16
HG = 4
GROUPS = HEADS // HG
CB = T // P
CHUNKS = BATCH * CB
STEPS = GROUPS * CHUNKS
KT = D // P
F = HG * DK
H = HG * M
CLAMP, EPS = 32.0, 1e-5
SCALE = DK ** -0.5
WQ, WK, WV, WG, WO = range(5)

F32 = mybir.dt.float32
F32R = mybir.dt.float32r
ALU = mybir.AluOpType
ACT = mybir.ActivationFunctionType
AX = mybir.AxisListType


def gated_slot_attention_block(nc, hs_cols, hs_rows, w_groups, ws1, ws2, gnorm, ffn_w, ffn_scale, ffn_bias,
                               rope_cos, rope_sin, keep_mask, below_mask, identity, out):
    with ExitStack() as ctx:
        def sb(name, cols, dt=F32):
            return ctx.enter_context(nc.sbuf_tensor(name, [P, cols], dt))

        def bank(name):
            return ctx.enter_context(nc.psum_tensor(name, [P, 512], F32))

        def sem(name):
            return ctx.enter_context(nc.semaphore(name))

        u_dram = nc.dram_tensor("u_scratch", (CHUNKS, P, P), F32, kind="Internal").ap()
        part_dram = nc.dram_tensor("part_scratch", (1 + STEPS, P, D), F32, kind="Internal").ap()

        w_hi = [sb(f"w_hi{m}", KT * F, F32R) for m in range(4)]
        w_lo = [sb(f"w_lo{m}", KT * F, F32R) for m in range(4)]
        wo_hi, wo_lo = sb("wo_hi", HG * D, F32R), sb("wo_lo", HG * D, F32R)
        w_raw = [sb(f"w_raw{s}", KT * F) for s in range(2)]
        ws2_part = sb("ws2_part", HEADS * M, F32R)
        gn = sb("gn", 1)
        cos_t, sin_t = sb("cos_t", CB * 64), sb("sin_t", CB * 128)
        keep, ident = sb("keep", P), sb("ident", P)
        keep_r, below_r = sb("keep_r", P, F32R), sb("below_r", P, F32R)
        minus_half = sb("minus_half", HG)
        hs_raw = [sb(f"hs_raw{s}", KT * P) for s in range(2)]
        hs_hi = [sb(f"hs_hi{s}", KT * P, F32R) for s in range(2)]
        hs_lo = [sb(f"hs_lo{s}", KT * P, F32R) for s in range(2)]
        u_part = [sb(f"u_part{s}", P, F32R) for s in range(2)]
        rope_a, rope_b, q_rot = sb("rope_a", F), sb("rope_b", F), sb("q_rot", F)
        k_rot = [sb(f"k_rot{s}", F) for s in range(2)]
        qT_hi, qT_lo = sb("qT_hi", F, F32R), sb("qT_lo", F, F32R)
        kT_hi, kT_lo = sb("kT_hi", F, F32R), sb("kT_lo", F, F32R)
        kn_hi, kn_lo = sb("kn_hi", F, F32R), sb("kn_lo", F, F32R)
        v_hi = [sb(f"v_hi{s}", F, F32R) for s in range(2)]
        v_lo = [sb(f"v_lo{s}", F, F32R) for s in range(2)]
        th = sb("th", F)
        gate = [sb(f"gate{s}", F) for s in range(2)]
        s_clip, es = sb("s_clip", H), sb("es", H)
        es_hi = [sb(f"es_hi{s}", H, F32R) for s in range(2)]
        es_lo = [sb(f"es_lo{s}", H, F32R) for s in range(2)]
        esT_hi, esT_lo = sb("esT_hi", H, F32R), sb("esT_lo", H, F32R)
        enz = sb("enz", H)
        masked = sb("masked", F)
        a_hi, a_lo = sb("a_hi", F, F32R), sb("a_lo", F, F32R)
        ok, prob, slot_p = sb("ok", H), sb("prob", H), sb("slot_p", H)
        ok_max, p_sum, sum_sq = sb("ok_max", HG), sb("p_sum", HG), sb("sum_sq", HG)
        eps_sum, var, rms = sb("eps_sum", HG), sb("var", HG), sb("rms", HG)
        pT_hi, pT_lo = sb("pT_hi", F, F32R), sb("pT_lo", F, F32R)
        s1_hi, s1_lo = sb("s1_hi", H, F32R), sb("s1_lo", H, F32R)
        s2_hi, s2_lo = sb("s2_hi", HG // 2 * DV, F32R), sb("s2_lo", HG // 2 * DV, F32R)
        o_sq, o_gated, o_norm = sb("o_sq", F), sb("o_gated", F), sb("o_norm", F)
        oT_hi, oT_lo = sb("oT_hi", F, F32R), sb("oT_lo", F, F32R)
        part = [sb(f"part{s}", D) for s in range(2)]

        bank_qv, bank_kg, bank_t, bank_a, bank_s, bank_c, bank_s2, bank_o = [
            bank(n) for n in ("bank_qv", "bank_kg", "bank_t", "bank_a", "bank_s", "bank_c", "bank_s2", "bank_o")]
        cums, s1_acc = bank_c[:, 0:H], bank_c[:, H:2 * H]

        wf_hi, wf_lo, wf_raw, wf_scaled = w_hi[0], w_lo[0], w_raw[1], w_raw[0]
        scale_row, bias_row = rope_a, rope_b
        x_parts = [w_hi[2][:, :].bitcast(F32), w_lo[2][:, :].bitcast(F32)]
        sum_a, sum_b, x_row, y_row = th, q_rot, o_sq, [o_gated, o_norm]
        x1 = k_rot
        x1T_hi, x1T_lo = [oT_hi, kn_hi], [oT_lo, kn_lo]
        z = gate
        stats, mean_var, shifted_var, rstd = sb("stats", 6), sb("mean_var", 2), sb("shifted_var", 1), sb("rstd", 1)
        stats2, mean_var2, shifted_var2, rstd2 = (
            sb("stats2", 6), sb("mean_var2", 2), sb("shifted_var2", 1), sb("rstd2", 1))

        const_in, pre_in, batch_in = sem("const_in"), sem("pre_in"), sem("batch_in")
        stored = [sem(f"stored{s}") for s in range(2)]
        hs_in, u_in = [sem(f"hs_in{s}") for s in range(2)], [sem(f"u_in{s}") for s in range(2)]
        w_in = [sem(f"w_in{s}") for s in range(2)]
        zeroed, ones_set, consts_made, ws2_made = sem("zeroed"), sem("ones_set"), sem("consts_made"), sem("ws2_made")
        u_mm, u_hi_made, u_made = sem("u_mm"), sem("u_hi_made"), sem("u_made")
        hs_hi_made, hs_lo_made = sem("hs_hi_made"), sem("hs_lo_made")
        w_hi_made, w_lo_made, wo_hi_made, wo_lo_made = (
            sem("w_hi_made"), sem("w_lo_made"), sem("wo_hi_made"), sem("wo_lo_made"))
        q_mm, k_mm, v_mm, g_mm, s_mm, out_mm = [sem(n) for n in ("q_mm", "k_mm", "v_mm", "g_mm", "s_mm", "out_mm")]
        a_mm, ok_mm, w2_mm, o_mm, s1_mm, s2_mm, cums_mm = [
            sem(n) for n in ("a_mm", "ok_mm", "w2_mm", "o_mm", "s1_mm", "s2_mm", "cums_mm")]
        qT_mm, kT_mm, pT_mm, esT_mm, oT_mm = [sem(n) for n in ("qT_mm", "kT_mm", "pT_mm", "esT_mm", "oT_mm")]
        q_turned, q_summed, k_turned, k_summed = [sem(n) for n in ("q_turned", "q_summed", "k_turned", "k_summed")]
        qT_hi_made, qT_lo_made, kT_hi_made, kT_lo_made, kn_hi_made, kn_lo_made, v_hi_made, v_lo_made = [
            sem(n) for n in ("qT_hi_made", "qT_lo_made", "kT_hi_made", "kT_lo_made", "kn_hi_made", "kn_lo_made",
                             "v_hi_made", "v_lo_made")]
        th_made, gate_made, s_clipped, es_made, es_hi_made, es_lo_made, esT_hi_made, esT_lo_made, enz_made = [
            sem(n) for n in ("th_made", "gate_made", "s_clipped", "es_made", "es_hi_made", "es_lo_made",
                             "esT_hi_made", "esT_lo_made", "enz_made")]
        a_masked, a_hi_made, a_lo_made, w2_masked, w2_hi_made, w2_lo_made = [
            sem(n) for n in ("a_masked", "a_hi_made", "a_lo_made", "w2_masked", "w2_hi_made", "w2_lo_made")]
        ok_scaled, ok_maxed, ok_shifted, prob_made, prob_summed, slot_p_made, pT_hi_made, pT_lo_made = [
            sem(n) for n in ("ok_scaled", "ok_maxed", "ok_shifted", "prob_made", "prob_summed", "slot_p_made",
                             "pT_hi_made", "pT_lo_made")]
        s1_hi_made, s1_lo_made, s2_hi_made, s2_lo_made = [
            sem(n) for n in ("s1_hi_made", "s1_lo_made", "s2_hi_made", "s2_lo_made")]
        o_squared, sq_summed, eps_scaled, var_made, rms_made, o_gated_made, o_norm_made = [
            sem(n) for n in ("o_squared", "sq_summed", "eps_scaled", "var_made", "rms_made", "o_gated_made",
                             "o_norm_made")]
        oT_hi_made, oT_lo_made, part_made = sem("oT_hi_made"), sem("oT_lo_made"), sem("part_made")
        wf_in, row_in, wf_scaled_made, wf_hi_made, wf_lo_made = [
            sem(n) for n in ("wf_in", "row_in", "wf_scaled_made", "wf_hi_made", "wf_lo_made")]
        x_in = [sem(f"x_in{s}") for s in range(2)]
        sum_a_made, sum_b_made, sum_c_made, x_made, stats_made, mean_made, shifted_made, rstd_made, x1_made = [
            sem(n) for n in ("sum_a_made", "sum_b_made", "sum_c_made", "x_made", "stats_made", "mean_made",
                             "shifted_made", "rstd_made", "x1_made")]
        biased_made, x1T_mm, x1T_hi_made, x1T_lo_made, ffn_mm, y_made = [
            sem(n) for n in ("biased_made", "x1T_mm", "x1T_hi_made", "x1T_lo_made", "ffn_mm", "y_made")]
        stats2_made, mean2_made, shifted2_made, rstd2_made, z_made = [
            sem(n) for n in ("stats2_made", "mean2_made", "shifted2_made", "rstd2_made", "z_made")]

        U_STORES = BATCH // 2
        LOOP_STORES = [U_STORES + STEPS // 2 + 1, U_STORES + STEPS // 2]

        def done(u, c, ahead=0):
            return u * CB + (c + 1 + ahead)

        def carried(u, c):
            return u * (CB - 1) + (c + 1)

        def all_steps(eng, body):
            with eng.Fori(0, GROUPS) as g:
                with eng.Fori(0, BATCH - 1) as b:
                    for c in range(CB):
                        body(g * BATCH + b, g, b, c, False)
                for c in range(CB):
                    body(g * BATCH + (BATCH - 1), g, BATCH - 1, c, True)

        SLOT = {WQ: 1, WK: 0, WV: 1, WG: 0, WO: 0}

        def raw_in(m, g, b=0):
            if m == WO:
                return g * 6 + b + 3
            return (g * 6 + (1 if m == WK else 2)) if SLOT[m] == 0 else (g * 2 + (1 if m == WQ else 2))

        def per_head(ap, n=HG):
            return ap.rearrange("p (h x) -> p h x", h=n)

        def over_heads(ap, n=HG):
            return ap.unsqueeze(1).broadcast_to([P, n, ap.shape[1]])

        def over_columns(ap, n):
            return ap.unsqueeze(2).broadcast_to([P, ap.shape[1], n])

        def of_pair(ap, half, n):
            return ap[64 * half:64 * half + 64, :].rearrange("p (r e x) -> p r e x", e=2, x=n)[:, :, half, :]

        def x_loads(j, s):
            return (j - s) * (5 * 16 // 2) + 5 * 16

        def last_phase(eng, front, back):
            front(0, 0)
            with eng.Fori(0, CHUNKS // 2 - 1) as jj:
                for s in range(2):
                    front(jj * 2 + (s + 1), 1 - s)
                    back(jj * 2 + s, s)
            front(CHUNKS - 1, 1)
            back(CHUNKS - 2, 0)
            back(CHUNKS - 1, 1)

        block = ctx.enter_context(nc.Block())

        @block.sync
        def _(sp):
            for dst, src in ((cos_t, rope_cos), (sin_t, rope_sin), (keep, keep_mask), (ident, identity), (gn, gnorm)):
                sp.dma_start(dst[:, :], src).then_inc(const_in, 16)
            sp.dma_start(w_raw[0][:, 0:KT * P], ws1).then_inc(pre_in, 16)
            sp.dma_start(w_raw[0][:, KT * P:KT * P + P], below_mask).then_inc(pre_in, 16)
            sp.dma_start(w_raw[0][:, 1024:2048], ws2).then_inc(pre_in, 16)
            for b in range(BATCH):
                if b:
                    sp.wait_ge(u_mm, b)
                for c in range(CB):
                    sp.dma_start(w_raw[1][:, :].rearrange("p (k c t) -> p k c t", k=KT, c=CB)[:, :, c, :],
                                 hs_cols[CB * b + c].rearrange("p (k t) -> p k t", k=KT)).then_inc(batch_in, 16)
                sp.wait_ge(u_made, b + 1)
                sp.dma_start(u_dram[CB * b:CB * b + CB].rearrange("c p t -> p c t"),
                             part[b % 2][:, :].rearrange("p (c t) -> p c t", c=CB)).then_inc(stored[b % 2], 16)
            for s in range(2):
                sp.wait_ge(stored[s], 16 * U_STORES)
            sp.wait_ge(ws2_made, 3)
            sp.wait_ge(consts_made, 2)

            def load_hs(slot, chunk):
                sp.dma_start(hs_raw[slot][:, :], hs_cols[chunk]).then_inc(hs_in[slot], 16)

            def load_u(slot, chunk):
                sp.dma_start(u_part[slot][:, :].bitcast(F32), u_dram[chunk]).then_inc(u_in[slot], 16)

            def load_w(m, g):
                sp.dma_start(w_raw[SLOT[m]][:, :], w_groups[g, m]).then_inc(w_in[SLOT[m]], 16)

            def w_split(count):
                sp.wait_ge(w_hi_made, count)
                sp.wait_ge(w_lo_made, count)

            for i in range(2):
                load_hs(i, i)
                load_u(i, i)
            load_w(WQ, 0)
            load_w(WK, 0)
            w_split(1)
            load_w(WV, 0)
            w_split(2)
            load_w(WG, 0)
            w_split(4)
            load_w(WO, 0)

            def step(u, g, b, c, last):
                chunk = c - 2 if last and c >= 2 else b * CB + (c + 2)
                sp.wait_ge(hs_hi_made, done(u, c))
                sp.wait_ge(hs_lo_made, done(u, c))
                load_hs(c % 2, chunk)
                sp.wait_ge(s_mm, done(u, c))
                load_u(c % 2, chunk)
                if c == 1:
                    sp.wait_ge(wo_hi_made, u + 1)
                    sp.wait_ge(wo_lo_made, u + 1)
                    if last:
                        load_w(WQ, (g + 1) % GROUPS)
                        load_w(WK, (g + 1) % GROUPS)
                    else:
                        load_w(WO, g)
                if c == 2 and last:
                    w_split(g * 4 + 5)
                    load_w(WV, (g + 1) % GROUPS)
                    w_split(g * 4 + 6)
                    load_w(WG, (g + 1) % GROUPS)
                sp.wait_ge(part_made, done(u, c))
                sp.dma_start(part_dram[u * CB + c], part[c % 2][:, :]).then_inc(stored[c % 2], 16)
                if c == 3 and last:
                    w_split(g * 4 + 8)
                    load_w(WO, (g + 1) % GROUPS)

            all_steps(sp, step)
            sp.wait_ge(part_made, STEPS + 1)
            sp.dma_start(part_dram[STEPS], part[0][:, :]).then_inc(stored[0], 16)
            sp.wait_ge(w_in[0], 16 * raw_in(WO, GROUPS))
            sp.wait_ge(o_norm_made, STEPS + 1)
            sp.wait_ge(gate_made, STEPS + 1)
            sp.dma_start(wf_raw[:, :], ffn_w).then_inc(wf_in, 16)
            sp.dma_start(scale_row[:, :], ffn_scale.partition_broadcast(P)).then_inc(row_in, 16)
            sp.dma_start(bias_row[:, :], ffn_bias.partition_broadcast(P)).then_inc(row_in, 16)
            sp.wait_ge(stored[0], 16 * LOOP_STORES[0])
            sp.wait_ge(stored[1], 16 * LOOP_STORES[1])
            sp.wait_ge(hs_hi_made, STEPS + 1)
            sp.wait_ge(hs_lo_made, STEPS + 1)

            def load_x(j, slot):
                sp.dma_start(hs_raw[slot][:, :], hs_rows[j]).then_inc(x_in[slot], 16)
                for g in range(GROUPS):
                    sp.dma_start(x_parts[slot][:, D * g:D * g + D], part_dram[j + (1 + g * CHUNKS)]
                                 ).then_inc(x_in[slot], 16)

            for s in range(2):
                sp.wait_ge(hs_in[s], 16 * (STEPS // 2 + 1))
                sp.wait_ge(u_in[s], 16 * (STEPS // 2 + 1))
                load_x(s, s)

            def row(j, s, more):
                if more:
                    sp.wait_ge(x_made, j + 1)
                    load_x(j + 2, s)
                sp.wait_ge(z_made, j + 1)
                sp.dma_start(out[j], z[s][:, :]).then_inc(stored[s], 16)

            with sp.Fori(0, CHUNKS // 2 - 1) as jj:
                for s in range(2):
                    row(jj * 2 + s, s, True)
            for s in range(2):
                row(CHUNKS - 2 + s, s, False)
            for s in range(2):
                sp.wait_ge(stored[s], 16 * (LOOP_STORES[s] + CHUNKS // 2))

        @block.gpsimd
        def _(pool):
            for t, value in ((part[0], 1.0), (part[1], 1.0)):
                pool.memset(t[:, :], value).then_inc(ones_set, 1)
            for t, value in ((pT_hi, 0.0), (pT_lo, 0.0), (wo_hi, 0.0), (wo_lo, 0.0)):
                pool.memset(t[:, :].bitcast(F32), value).then_inc(zeroed, 1)
            pool.memset(o_gated[:, :], 0.0).then_inc(o_gated_made, 1)
            pool.memset(var[:, :], 1.0).then_inc(var_made, 1)
            pool.memset(minus_half[:, :], -0.5).then_inc(zeroed, 1)

            def hs_split(slot, n):
                pool.wait_ge(hs_hi_made, n)
                pool.tensor_tensor(hs_lo[slot][:, :], hs_raw[slot][:, :], hs_hi[slot][:, :].bitcast(F32),
                                   ALU.subtract).then_inc(hs_lo_made, 1)

            def q_sum(n):
                pool.wait_ge(q_turned, n)
                pool.tensor_tensor(q_rot[:, :], rope_a[:, :], rope_b[:, :], ALU.add).then_inc(q_summed, 1)

            def k_sum(slot, n):
                pool.wait_ge(k_turned, n)
                pool.tensor_tensor(k_rot[slot][:, :], rope_a[:, :], rope_b[:, :], ALU.add).then_inc(k_summed, 1)

            def es_split(slot, n):
                pool.wait_ge(es_hi_made, n)
                pool.tensor_tensor(es_lo[slot][:, :], es[:, :], es_hi[slot][:, :].bitcast(F32),
                                   ALU.subtract).then_inc(es_lo_made, 1)

            def a_split(n):
                pool.wait_ge(a_hi_made, n)
                pool.tensor_tensor(a_lo[:, :], masked[:, :], a_hi[:, :].bitcast(F32),
                                   ALU.subtract).then_inc(a_lo_made, 1)

            hs_split(0, 1)
            q_sum(1)
            k_sum(0, 1)
            es_split(0, 1)
            a_split(1)
            hs_split(1, 2)
            pool.wait_ge(zeroed, 5)

            def step(u, g, b, c, last):
                pool.wait_ge(o_gated_made, done(u, c))
                pool.wait_ge(var_made, done(u, c))
                pool.tensor_tensor(rms[:, :], var[:, :], minus_half[:, :], ALU.pow).then_inc(rms_made, 1)
                pool.wait_ge(rms_made, done(u, c))
                pool.tensor_tensor(per_head(o_norm[:, :]), per_head(o_gated[:, :]), over_columns(rms[:, :], DV),
                                   ALU.mult).then_inc(o_norm_made, 1)
                q_sum(done(u, c, 1))
                pool.wait_ge(ok_maxed, done(u, c))
                pool.tensor_tensor(per_head(ok[:, :]), per_head(ok[:, :]), over_columns(ok_max[:, :], M),
                                   ALU.subtract).then_inc(ok_shifted, 1)
                if c < CB - 1:
                    pool.wait_ge(kn_hi_made, carried(u, c))
                    pool.tensor_tensor(kn_lo[:, :], k_rot[c % 2][:, :], kn_hi[:, :].bitcast(F32),
                                       ALU.subtract).then_inc(kn_lo_made, 1)
                pool.wait_ge(prob_made, done(u, c))
                pool.tensor_tensor(slot_p[:, :], prob[:, :], enz[:, :], ALU.mult).then_inc(slot_p_made, 1)
                k_sum((c + 1) % 2, done(u, c, 1))
                es_split((c + 1) % 2, done(u, c, 1))
                pool.wait_ge(w2_hi_made, done(u, c))
                pool.tensor_tensor(a_lo[:, :], masked[:, :], a_hi[:, :].bitcast(F32),
                                   ALU.subtract).then_inc(w2_lo_made, 1)
                hs_split(c % 2, done(u, c, 2))
                a_split(done(u, c, 1))

            all_steps(pool, step)
            pool.wait_ge(o_gated_made, STEPS + 1)
            pool.wait_ge(var_made, STEPS + 1)
            pool.tensor_tensor(rms[:, :], var[:, :], minus_half[:, :], ALU.pow).then_inc(rms_made, 1)
            pool.wait_ge(rms_made, STEPS + 1)
            pool.tensor_tensor(per_head(o_norm[:, :]), per_head(o_gated[:, :]), over_columns(rms[:, :], DV),
                               ALU.mult).then_inc(o_norm_made, 1)

            def front(j, s):
                if not (isinstance(j, int) and j == 0):
                    pool.wait_ge(x_made, j)
                pool.wait_ge(x_in[s], x_loads(j, s))
                pool.tensor_tensor(sum_a[:, :], x_parts[s][:, 0:D], x_parts[s][:, D:2 * D], ALU.add
                                   ).then_inc(sum_a_made, 1)
                pool.wait_ge(shifted_made, j + 1)
                pool.tensor_tensor(rstd[:, :], shifted_var[:, :], minus_half[:, 0:1], ALU.pow).then_inc(rstd_made, 1)
                pool.wait_ge(x1_made, j + 1)
                pool.wait_ge(row_in, 32)
                pool.wait_ge(x1T_mm, j + 1)
                pool.tensor_tensor(x1[s][:, :], x1[s][:, :], bias_row[:, :], ALU.add).then_inc(biased_made, 1)

            def back(j, s):
                pool.wait_ge(shifted2_made, j + 1)
                pool.tensor_tensor(rstd2[:, :], shifted_var2[:, :], minus_half[:, 0:1], ALU.pow
                                   ).then_inc(rstd2_made, 1)

            last_phase(pool, front, back)

        @block.scalar
        def _(act):
            def copy(dst, src, scale=1.0):
                return act.activation(dst, src, ACT.Copy, scale=scale)

            act.wait_ge(const_in, 16 * 5)
            copy(keep_r[:, :], keep[:, :]).then_inc(consts_made, 1)
            act.wait_ge(pre_in, 16 * 3)
            copy(below_r[:, :], w_raw[0][:, KT * P:KT * P + P]).then_inc(consts_made, 1)
            copy(ws2_part[0:64, :], w_raw[0][0:64, 1024:2048]).then_inc(ws2_made, 1)
            copy(w_hi[0][64:128, 0:1024], w_raw[0][64:128, 1024:2048]).then_inc(ws2_made, 1)
            act.wait_ge(ones_set, 2)
            for b in range(BATCH):
                act.wait_ge(u_mm, b + 1)
                if b >= 2:
                    act.wait_ge(stored[b % 2], 16 * (b // 2))
                if b:
                    act.wait_ge(u_made, b)
                copy(rope_a[:, :].bitcast(F32R), bank_qv[:, :])
                copy(part[b % 2][0:RANK, :].bitcast(F32R), bank_qv[0:RANK, :])
                copy(part[b % 2][64:64 + RANK, :].bitcast(F32R), bank_qv[64:64 + RANK, :]).then_inc(u_hi_made, 1)

            def w_split(m, loads):
                act.wait_ge(w_in[SLOT[m]], 16 * loads)
                copy(w_hi[m][:, :], w_raw[SLOT[m]][:, :]).then_inc(w_hi_made, 1)

            def hs_split(slot, n_in):
                act.wait_ge(hs_in[slot], n_in)
                copy(hs_hi[slot][:, :], hs_raw[slot][:, :]).then_inc(hs_hi_made, 1)

            def exp_s(slot, n):
                act.wait_ge(s_clipped, n)
                act.activation(es[:, :], s_clip[:, :], ACT.Exp).then_inc(es_made, 1)
                act.wait_ge(es_made, n)
                copy(es_hi[slot][:, :], es[:, :]).then_inc(es_hi_made, 1)

            def from_bank(dst, src, wait, n, made):
                act.wait_ge(wait, n)
                copy(dst, src).then_inc(made, 1)

            hs_split(0, 16)
            act.wait_ge(ws2_made, 3)
            for m in (WQ, WK, WV, WG):
                w_split(m, raw_in(m, 0))
            act.wait_ge(zeroed, 5)
            from_bank(qT_hi[:, :], bank_t[:, :], qT_mm, 1, qT_hi_made)
            exp_s(0, 1)
            from_bank(v_hi[0][:, :], bank_qv[:, :], v_mm, 1, v_hi_made)
            from_bank(esT_hi[:, :], bank_t[:, 0:H], esT_mm, 1, esT_hi_made)
            act.wait_ge(g_mm, 1)
            act.activation(th[:, :], bank_kg[:, :], ACT.Tanh, scale=0.5).then_inc(th_made, 1)
            from_bank(kT_hi[:, :], bank_t[:, :], kT_mm, 1, kT_hi_made)
            hs_split(1, 16)
            act.wait_ge(a_masked, 1)
            copy(a_hi[:, :], masked[:, :]).then_inc(a_hi_made, 1)

            def step(u, g, b, c, last):
                i, n = done(u, c), done(u, c, 1)
                act.wait_ge(ok_shifted, i)
                act.activation(prob[:, :], ok[:, :], ACT.Exp).then_inc(prob_made, 1)
                if last and c == 2:
                    act.wait_ge(q_mm, n)
                    w_split(WQ, g * 2 + 3)
                from_bank(qT_hi[:, :], bank_t[:, :], qT_mm, n, qT_hi_made)
                from_bank(oT_hi[:, :], bank_t[:, :], oT_mm, i, oT_hi_made)
                exp_s((c + 1) % 2, n)
                if c < CB - 1:
                    act.wait_ge(k_summed, done(u, c))
                    copy(kn_hi[:, :], k_rot[c % 2][:, :]).then_inc(kn_hi_made, 1)
                if last and c == 2:
                    act.wait_ge(k_mm, n)
                    w_split(WK, g * 6 + 7)
                from_bank(v_hi[(c + 1) % 2][:, :], bank_qv[:, :], v_mm, n, v_hi_made)
                act.wait_ge(pT_mm, i)
                copy(of_pair(pT_hi[:, :], 0, P), per_head(bank_t[0:64, 0:H], 2))
                copy(of_pair(pT_hi[:, :], 1, P), per_head(bank_t[64:128, 0:H], 2)).then_inc(pT_hi_made, 1)
                if last and c == 2:
                    w_split(WV, g * 2 + 4)
                act.wait_ge(out_mm, i)
                act.wait_ge(stored[c % 2], (u * (CB // 2) + (c // 2 + U_STORES)) * 16)
                copy(part[c % 2][:, :], bank_o[:, :]).then_inc(part_made, 1)
                if c == 0:
                    act.wait_ge(w_in[0], (g * 6 + b + 3) * 16)
                    copy(wo_hi[:, :], w_raw[0][:, :], gn[:, 0:1]).then_inc(wo_hi_made, 1)
                from_bank(esT_hi[:, :], bank_t[:, 0:H], esT_mm, n, esT_hi_made)
                act.wait_ge(w2_masked, i)
                copy(a_hi[:, :], masked[:, :]).then_inc(w2_hi_made, 1)
                act.wait_ge(g_mm, n)
                act.activation(th[:, :], bank_kg[:, :], ACT.Tanh, scale=0.5).then_inc(th_made, 1)
                from_bank(kT_hi[:, :], bank_t[:, :], kT_mm, n, kT_hi_made)
                hs_split(c % 2, (u * (CB // 2) + (c // 2 + 2)) * 16)
                if last and c == 2:
                    w_split(WG, g * 6 + 8)
                act.wait_ge(o_mm, i)
                act.activation(o_sq[:, :], bank_o[:, :], ACT.Square).then_inc(o_squared, 1)
                if c < CB - 1:
                    from_bank(s1_hi[:, :], s1_acc, s1_mm, carried(u, c), s1_hi_made)
                    act.wait_ge(s2_mm, carried(u, c))
                    copy(per_head(s2_hi[0:64, :], 2), of_pair(bank_s2[:, :], 0, DV))
                    copy(per_head(s2_hi[64:128, :], 2), of_pair(bank_s2[:, :], 1, DV)).then_inc(s2_hi_made, 1)
                act.wait_ge(a_masked, n)
                copy(a_hi[:, :], masked[:, :]).then_inc(a_hi_made, 1)

            all_steps(act, step)
            from_bank(oT_hi[:, :], bank_t[:, :], oT_mm, STEPS + 1, oT_hi_made)
            act.wait_ge(out_mm, STEPS + 1)
            act.wait_ge(stored[0], (STEPS // 2 + U_STORES) * 16)
            copy(part[0][:, :], bank_o[:, :]).then_inc(part_made, 1)

            act.wait_ge(wf_scaled_made, KT)
            copy(wf_hi[:, :], wf_scaled[:, :]).then_inc(wf_hi_made, 1)

            def front(j, s):
                act.wait_ge(x1T_mm, j + 1)
                copy(x1T_hi[s][:, :], bank_t[:, :]).then_inc(x1T_hi_made, 1)

            last_phase(act, front, lambda j, s: None)

        @block.vector
        def _(dve):
            def minus_hi(dst, src, hi):
                return dve.tensor_tensor(dst, src, hi.bitcast(F32), ALU.subtract)

            dve.wait_ge(ws2_made, 2)
            minus_hi(ws2_part[64:128, :], w_raw[0][64:128, 1024:2048], w_hi[0][64:128, 0:1024]).then_inc(ws2_made, 1)
            for b in range(BATCH):
                dve.wait_ge(u_hi_made, b + 1)
                for q in (32, 96):
                    last = minus_hi(part[b % 2][q:q + RANK, :].bitcast(F32R), bank_qv[q:q + RANK, :],
                                    rope_a[q:q + RANK, :])
                last.then_inc(u_made, 1)

            def rotate(chunk, bank_in, turned, n):
                halves = "p (r x) -> p r x"
                x = bank_in[:, :].rearrange(halves, x=DK // 2)
                dve.tensor_tensor(rope_a[:, :].rearrange(halves, x=DK // 2), x,
                                  over_heads(cos_t[:, 64 * chunk:64 * chunk + 64], 2 * HG), ALU.mult)
                sins = sin_t[:, 128 * chunk:128 * chunk + 128]
                for half in range(2):
                    x = bank_in[:, :].rearrange("p (h e x) -> p h e x", e=2, x=DK // 2)[:, :, 1 - half, :]
                    y = rope_b[:, :].rearrange("p (h e x) -> p h e x", e=2, x=DK // 2)[:, :, half, :]
                    last = dve.tensor_tensor(y, x, over_heads(sins[:, 64 * half:64 * half + 64]), ALU.mult)
                last.then_inc(turned, 1)

            def rotate_q(chunk, n, first=False):
                dve.wait_ge(q_mm, n)
                if not first:
                    dve.wait_ge(k_summed, n - 1)
                rotate(chunk, bank_qv, q_turned, n)

            def rotate_k(chunk, n):
                dve.wait_ge(k_mm, n)
                dve.wait_ge(q_summed, n)
                rotate(chunk, bank_kg, k_turned, n)

            def w_split(m, n):
                dve.wait_ge(w_hi_made, n)
                minus_hi(w_lo[m][:, :], w_raw[SLOT[m]][:, :], w_hi[m][:, :]).then_inc(w_lo_made, 1)

            def lo(dst, src, hi, hi_made, n, made):
                dve.wait_ge(hi_made, n)
                minus_hi(dst, src, hi).then_inc(made, 1)

            def clip(n):
                dve.wait_ge(s_mm, n)
                dve.tensor_scalar(s_clip[:, :], bank_s[:, 0:H], CLAMP, -CLAMP, ALU.min, ALU.max).then_inc(s_clipped, 1)

            def make_gate(slot, n):
                dve.wait_ge(th_made, n)
                dve.scalar_tensor_tensor(gate[slot][:, :], th[:, :], 1.0, bank_kg[:, :], ALU.add, ALU.mult
                                         ).then_inc(gate_made, 1)

            def make_enz(n):
                dve.wait_ge(cums_mm, n)
                dve.reciprocal(enz[:, :], cums).then_inc(enz_made, 1)

            def mask(mm, n, made):
                dve.wait_ge(mm, n)
                dve.tensor_tensor(per_head(masked[:, :]), per_head(bank_a[:, :]), over_heads(keep[:, :]), ALU.mult
                                  ).then_inc(made, 1)

            dve.wait_ge(const_in, 16 * 5)
            for m in (WQ, WK, WV, WG):
                w_split(m, m + 1)
            rotate_q(0, 1, first=True)
            rotate_k(0, 1)
            lo(qT_lo[:, :], bank_t[:, :], qT_hi[:, :], qT_hi_made, 1, qT_lo_made)
            clip(1)
            lo(v_lo[0][:, :], bank_qv[:, :], v_hi[0][:, :], v_hi_made, 1, v_lo_made)
            lo(esT_lo[:, :], bank_t[:, 0:H], esT_hi[:, :], esT_hi_made, 1, esT_lo_made)
            make_gate(0, 1)
            lo(kT_lo[:, :], bank_t[:, :], kT_hi[:, :], kT_hi_made, 1, kT_lo_made)
            make_enz(1)
            mask(a_mm, 1, a_masked)
            dve.wait_ge(zeroed, 5)

            def step(u, g, b, c, last):
                i, n = done(u, c), done(u, c, 1)
                rotate_q((c + 1) % CB, n)
                dve.wait_ge(ok_mm, i)
                dve.scalar_tensor_tensor(ok[:, :], bank_s[:, 0:H], SCALE, enz[:, :], ALU.mult, ALU.mult
                                         ).then_inc(ok_scaled, 1)
                dve.wait_ge(ok_scaled, i)
                dve.tensor_reduce(ok_max[:, :], per_head(ok[:, :]), AX.X, ALU.max).then_inc(ok_maxed, 1)
                dve.wait_ge(prob_made, i)
                dve.tensor_reduce(p_sum[:, :], per_head(prob[:, :]), AX.X, ALU.add).then_inc(prob_summed, 1)
                if last and c == 2:
                    w_split(WQ, g * 4 + 5)
                rotate_k((c + 1) % CB, n)
                lo(qT_lo[:, :], bank_t[:, :], qT_hi[:, :], qT_hi_made, n, qT_lo_made)
                clip(n)
                lo(oT_lo[:, :], bank_t[:, :], oT_hi[:, :], oT_hi_made, i, oT_lo_made)
                if last and c == 2:
                    w_split(WK, g * 4 + 6)
                lo(v_lo[(c + 1) % 2][:, :], bank_qv[:, :], v_hi[(c + 1) % 2][:, :], v_hi_made, n, v_lo_made)
                dve.wait_ge(pT_hi_made, i)
                for half in range(2):
                    r = slice(64 * half, 64 * half + 64)
                    x = minus_hi(of_pair(pT_lo[:, :], half, P), per_head(bank_t[r, 0:H], 2),
                                 of_pair(pT_hi[:, :], half, P))
                x.then_inc(pT_lo_made, 1)
                dve.wait_ge(prob_summed, i)
                dve.scalar_tensor_tensor(eps_sum[:, :], p_sum[:, :], 4 * EPS, p_sum[:, :], ALU.mult, ALU.mult
                                         ).then_inc(eps_scaled, 1)
                if last and c == 2:
                    w_split(WV, g * 4 + 7)
                if c == 0:
                    dve.wait_ge(wo_hi_made, u + 1)
                    dve.scalar_tensor_tensor(wo_lo[:, :], w_raw[0][:, :], gn[:, 0:1], wo_hi[:, :].bitcast(F32),
                                             ALU.mult, ALU.subtract).then_inc(wo_lo_made, 1)
                mask(w2_mm, i, w2_masked)
                lo(esT_lo[:, :], bank_t[:, 0:H], esT_hi[:, :], esT_hi_made, n, esT_lo_made)
                make_gate((c + 1) % 2, n)
                lo(kT_lo[:, :], bank_t[:, :], kT_hi[:, :], kT_hi_made, n, kT_lo_made)
                make_enz(n)
                if last and c == 2:
                    w_split(WG, g * 4 + 8)
                dve.wait_ge(o_squared, i)
                dve.wait_ge(o_norm_made, i)
                dve.tensor_tensor(o_gated[:, :], bank_o[:, :], gate[c % 2][:, :], ALU.mult).then_inc(o_gated_made, 1)
                dve.tensor_reduce(sum_sq[:, :], per_head(o_sq[:, :]), AX.X, ALU.add).then_inc(sq_summed, 1)
                dve.wait_ge(sq_summed, i)
                dve.wait_ge(eps_scaled, i)
                dve.scalar_tensor_tensor(var[:, :], sum_sq[:, :], 4.0 / DV, eps_sum[:, :], ALU.mult, ALU.add
                                         ).then_inc(var_made, 1)
                if c < CB - 1:
                    lo(s1_lo[:, :], s1_acc, s1_hi[:, :], s1_hi_made, carried(u, c), s1_lo_made)
                    dve.wait_ge(s2_hi_made, carried(u, c))
                    for half in range(2):
                        r = slice(64 * half, 64 * half + 64)
                        x = minus_hi(per_head(s2_lo[r, :], 2), of_pair(bank_s2[:, :], half, DV), per_head(s2_hi[r, :], 2))
                    x.then_inc(s2_lo_made, 1)
                mask(a_mm, n, a_masked)

            all_steps(dve, step)
            lo(oT_lo[:, :], bank_t[:, :], oT_hi[:, :], oT_hi_made, STEPS + 1, oT_lo_made)

            dve.wait_ge(wf_in, 16)
            dve.wait_ge(row_in, 32)
            for k in range(KT):
                cols = slice(D * k, D * k + D)
                dve.tensor_tensor(wf_scaled[:, cols], wf_raw[:, cols], scale_row[:, :], ALU.mult
                                  ).then_inc(wf_scaled_made, 1)
            dve.wait_ge(wf_hi_made, 1)
            minus_hi(wf_lo[:, :], wf_scaled[:, :], wf_hi[:, :]).then_inc(wf_lo_made, 1)

            def norm(x, dst, j, st, mv, sh, rs, made, m_stats, m_mean, m_shift, m_rstd, m_dst):
                dve.wait_ge(made, j + 1)
                dve.bn_stats(st[:, :], x).then_inc(m_stats, 1)
                dve.wait_ge(const_in, 16 * 5)
                dve.wait_ge(m_stats, j + 1)
                dve.bn_aggr(mv[:, :], st[:, :]).then_inc(m_mean, 1)
                dve.wait_ge(m_mean, j + 1)
                dve.tensor_scalar(sh[:, :], mv[:, 1:2], EPS, None, ALU.add).then_inc(m_shift, 1)
                dve.wait_ge(m_rstd, j + 1)
                dve.tensor_scalar(dst, x, mv[:, 0:1], rs[:, 0:1], ALU.subtract, ALU.mult).then_inc(m_dst, 1)

            def front(j, s):
                dve.wait_ge(x_in[s], x_loads(j, s))
                dve.tensor_tensor(sum_b[:, :], x_parts[s][:, 2 * D:3 * D], x_parts[s][:, 3 * D:4 * D], ALU.add
                                  ).then_inc(sum_b_made, 1)
                dve.wait_ge(sum_b_made, j + 1)
                dve.tensor_tensor(x_row[:, :], sum_b[:, :], hs_raw[s][:, :], ALU.add).then_inc(sum_c_made, 1)
                dve.wait_ge(sum_c_made, j + 1)
                dve.wait_ge(sum_a_made, j + 1)
                dve.tensor_tensor(x_row[:, :], x_row[:, :], sum_a[:, :], ALU.add).then_inc(x_made, 1)
                norm(x_row[:, :], x1[s][:, :], j, stats, mean_var, shifted_var, rstd, x_made, stats_made, mean_made,
                     shifted_made, rstd_made, x1_made)
                lo(x1T_lo[s][:, :], bank_t[:, :], x1T_hi[s][:, :], x1T_hi_made, j + 1, x1T_lo_made)

            def back(j, s):
                dve.wait_ge(ffn_mm, j + 1)
                dve.wait_ge(biased_made, j + 1)
                dve.tensor_tensor(y_row[s][:, :], bank_o[:, :], x1[s][:, :], ALU.add).then_inc(y_made, 1)
                dve.wait_ge(stored[s], (j - s) * (16 // 2) + 16 * LOOP_STORES[s])
                norm(y_row[s][:, :], z[s][:, :], j, stats2, mean_var2, shifted_var2, rstd2, y_made, stats2_made,
                     mean2_made, shifted2_made, rstd2_made, z_made)

            last_phase(dve, front, back)

        @block.tensor
        def _(pe):
            def product(dst, lhs, rhs, start=True, stop=True, **kw):
                for n, (x, y) in enumerate(((lhs[0], rhs[0]), (lhs[0], rhs[1]), (lhs[1], rhs[0]))):
                    mm = pe.matmul(dst, x, y, start=start and n == 0, stop=stop and n == 2, **kw)
                return mm

            def cols(pair, a, n):
                return tuple(t[:, a:a + n] for t in pair)

            def project(m, dst, slot):
                for k in range(KT):
                    mm = product(dst[:, :], cols((hs_hi[slot], hs_lo[slot]), P * k, P),
                                 cols((w_hi[m], w_lo[m]), F * k, F), start=k == 0, stop=k == KT - 1)
                return mm

            def transposes(src, n=HG):
                for h in range(n):
                    mm = pe.transpose(bank_t[:, P * h:P * h + P], src[:, P * h:P * h + P], ident[:, :])
                return mm

            def w_ready(n):
                pe.wait_ge(w_hi_made, n)
                pe.wait_ge(w_lo_made, n)

            def running_sum(slot, n, first):
                pe.wait_ge(es_hi_made, n)
                pe.wait_ge(es_lo_made, n)
                if not first:
                    for t in (es_hi, es_lo):
                        pe.matmul(cums, below_r[:, :], t[1 - slot][:, :], start=False, stop=False,
                                  skip_group_check=True)
                pe.matmul(cums, keep_r[:, :], es_hi[slot][:, :], start=first, stop=False, skip_group_check=True)
                pe.matmul(cums, keep_r[:, :], es_lo[slot][:, :], start=False, stop=True, skip_group_check=True
                          ).then_inc(cums_mm, 1)

            def scores(n):
                pe.wait_ge(kT_hi_made, n)
                pe.wait_ge(kT_lo_made, n)
                for h in range(HG):
                    mm = product(bank_a[:, P * h:P * h + P], cols((kT_hi, kT_lo), P * h, P),
                                 cols((qT_hi, qT_lo), P * h, P))
                mm.then_inc(a_mm, 1)

            pe.wait_ge(const_in, 16 * 5)
            pe.wait_ge(pre_in, 16 * 3)
            for b in range(BATCH):
                pe.wait_ge(batch_in, 16 * CB * (b + 1))
                if b:
                    pe.wait_ge(u_made, b)
                for k in range(KT):
                    mm = pe.matmul(bank_qv[:, :], w_raw[0][:, P * k:P * k + P], w_raw[1][:, T * k:T * k + T],
                                   start=k == 0, stop=k == KT - 1)
                mm.then_inc(u_mm, 1)
            pe.wait_ge(u_made, BATCH)
            pe.wait_ge(consts_made, 2)
            pe.wait_ge(hs_hi_made, 1)
            pe.wait_ge(hs_lo_made, 1)
            w_ready(1)
            project(WQ, bank_qv, 0).then_inc(q_mm, 1)
            w_ready(2)
            project(WK, bank_kg, 0).then_inc(k_mm, 1)
            pe.wait_ge(q_summed, 1)
            transposes(q_rot).then_inc(qT_mm, 1)
            pe.wait_ge(u_in[0], 16)
            pe.matmul(bank_s[:, 0:H], u_part[0][:, :], ws2_part[:, 0:H], start=True, stop=True).then_inc(s_mm, 1)
            w_ready(3)
            project(WV, bank_qv, 0).then_inc(v_mm, 1)
            pe.wait_ge(qT_lo_made, 1)
            pe.wait_ge(es_made, 1)
            transposes(es, HG // 2).then_inc(esT_mm, 1)
            w_ready(4)
            pe.wait_ge(k_turned, 1)
            project(WG, bank_kg, 0).then_inc(g_mm, 1)
            pe.wait_ge(k_summed, 1)
            pe.wait_ge(esT_lo_made, 1)
            transposes(k_rot[0]).then_inc(kT_mm, 1)
            running_sum(0, 1, True)
            scores(1)

            def step(u, g, b, c, last):
                i, n = done(u, c), done(u, c, 1)
                now, nxt = c % 2, (c + 1) % 2
                w_set = (g * 4 + 8) if last and c == CB - 1 else g * 4 + 4
                pe.wait_ge(hs_hi_made, n)
                pe.wait_ge(hs_lo_made, n)
                pe.wait_ge(v_lo_made, i)
                if last and c == CB - 1:
                    w_ready(g * 4 + 5)
                project(WQ, bank_qv, nxt).then_inc(q_mm, 1)
                pe.wait_ge(a_hi_made, i)
                pe.wait_ge(a_lo_made, i)
                if c:
                    pe.wait_ge(s1_hi_made, carried(u, c - 1))
                    pe.wait_ge(s1_lo_made, carried(u, c - 1))
                for h in range(HG):
                    mm = product(bank_s[:, M * h:M * h + M], cols((a_hi, a_lo), P * h, P),
                                 cols((es_hi[now], es_lo[now]), M * h, M), stop=c == 0)
                    if c:
                        mm = product(bank_s[:, M * h:M * h + M], cols((qT_hi, qT_lo), P * h, P),
                                     cols((s1_hi, s1_lo), M * h, M), start=False)
                mm.then_inc(ok_mm, 1)
                pe.wait_ge(gate_made, i)
                if last and c == CB - 1:
                    w_ready(g * 4 + 6)
                project(WK, bank_kg, nxt).then_inc(k_mm, 1)
                pe.wait_ge(q_summed, n)
                transposes(q_rot).then_inc(qT_mm, 1)
                pe.wait_ge(ok_scaled, i)
                pe.wait_ge(u_in[nxt], (u * 2 + ((c + 1) // 2 + 1)) * 16)
                pe.matmul(bank_s[:, 0:H], u_part[nxt][:, :], ws2_cols(g, last and c == CB - 1), start=True,
                          stop=True).then_inc(s_mm, 1)
                pe.wait_ge(o_norm_made, i)
                pe.wait_ge(qT_lo_made, n)
                transposes(o_norm).then_inc(oT_mm, 1)
                pe.wait_ge(q_turned, n)
                if last and c == CB - 1:
                    w_ready(g * 4 + 7)
                project(WV, bank_qv, nxt).then_inc(v_mm, 1)
                pe.wait_ge(slot_p_made, i)
                pe.wait_ge(oT_lo_made, i)
                transposes(slot_p, HG // 2).then_inc(pT_mm, 1)
                if c == 1:
                    pe.wait_ge(wo_hi_made, u + 1)
                    pe.wait_ge(wo_lo_made, u + 1)
                for h in range(HG):
                    mm = product(bank_o[:, :], cols((oT_hi, oT_lo), P * h, P), cols((wo_hi, wo_lo), D * h, D),
                                 start=h == 0, stop=h == HG - 1)
                mm.then_inc(out_mm, 1)
                pe.wait_ge(pT_lo_made, i)
                for r in range(HG // 2):
                    mm = product(bank_a[:, 2 * P * r:2 * P * r + 2 * P], cols((esT_hi, esT_lo), P * r, P),
                                 cols((pT_hi, pT_lo), 2 * P * r, 2 * P))
                mm.then_inc(w2_mm, 1)
                pe.wait_ge(es_made, n)
                transposes(es, HG // 2).then_inc(esT_mm, 1)
                pe.wait_ge(k_turned, n)
                if last and c == CB - 1:
                    w_ready(g * 4 + 8)
                project(WG, bank_kg, nxt).then_inc(g_mm, 1)
                pe.wait_ge(k_summed, n)
                pe.wait_ge(esT_lo_made, n)
                transposes(k_rot[nxt]).then_inc(kT_mm, 1)
                running_sum(nxt, n, c == CB - 1)
                pe.wait_ge(w2_lo_made, i)
                pe.wait_ge(part_made, i)
                if c:
                    pe.wait_ge(s2_hi_made, carried(u, c - 1))
                    pe.wait_ge(s2_lo_made, carried(u, c - 1))
                for h in range(HG):
                    dst = bank_o[:, DV * h:DV * h + DV]
                    mm = product(dst, cols((a_hi, a_lo), P * h, P), cols((v_hi[now], v_lo[now]), DV * h, DV),
                                 stop=c == 0)
                    if c:
                        mm = product(dst, cols((pT_hi, pT_lo), P * h, P),
                                     cols((s2_hi, s2_lo), DV * (h // 2), DV), start=False)
                mm.then_inc(o_mm, 1)
                if c < CB - 1:
                    pe.wait_ge(kn_lo_made, carried(u, c))
                    pe.wait_ge(enz_made, n)
                    for h in range(HG):
                        mm = product(s1_acc[:, M * h:M * h + M], cols((kn_hi, kn_lo), P * h, P),
                                     cols((es_hi[now], es_lo[now]), M * h, M), start=False, skip_group_check=True)
                    mm.then_inc(s1_mm, 1)
                    for r in range(HG // 2):
                        mm = product(bank_s2[:, 2 * DV * r:2 * DV * r + 2 * DV],
                                     cols((es_hi[now], es_lo[now]), P * r, P),
                                     cols((v_hi[now], v_lo[now]), 2 * DV * r, 2 * DV),
                                     start=c == 0 and r == 0, skip_group_check=True)
                    mm.then_inc(s2_mm, 1)
                scores(n)

            def ws2_cols(g, next_group):
                g = (g + 1) % GROUPS if next_group else g
                return ws2_part[:, bass.ds(g * H, H)]

            all_steps(pe, step)
            pe.wait_ge(o_norm_made, STEPS + 1)
            transposes(o_norm).then_inc(oT_mm, 1)
            pe.wait_ge(oT_lo_made, STEPS + 1)
            for h in range(HG):
                mm = product(bank_o[:, :], cols((oT_hi, oT_lo), P * h, P), cols((wo_hi, wo_lo), D * h, D),
                             start=h == 0, stop=h == HG - 1)
            mm.then_inc(out_mm, 1)

            def front(j, s):
                pe.wait_ge(x1_made, j + 1)
                if not (isinstance(j, int) and j == 0):
                    pe.wait_ge(x1T_lo_made, j)
                transposes(x1[s]).then_inc(x1T_mm, 1)

            def back(j, s):
                pe.wait_ge(x1T_lo_made, j + 1)
                pe.wait_ge(wf_lo_made, 1)
                if not (isinstance(j, int) and j == 0):
                    pe.wait_ge(y_made, j)
                for k in range(KT):
                    mm = product(bank_o[:, :], cols((x1T_hi[s], x1T_lo[s]), P * k, P), cols((wf_hi, wf_lo), D * k, D),
                                 start=k == 0, stop=k == KT - 1)
                mm.then_inc(ffn_mm, 1)

            last_phase(pe, front, back)


def kernel(**inputs):
    import numpy as np
    import concourse.bacc as bacc
    from concourse.bass_utils import run_bass_kernel_spmd

    def arr(name):
        return np.ascontiguousarray(inputs[name])

    hs = arr("L0_attn_hidden_states").reshape(CHUNKS, P, D)
    hs_cols = hs.reshape(CHUNKS, P, KT, P).transpose(0, 3, 2, 1).reshape(CHUNKS, P, KT * P)

    def grouped(w):
        return w.reshape(GROUPS, F, KT, P).transpose(0, 3, 2, 1).reshape(GROUPS, P, KT * F)

    wo = arr("L0_attn_Wo").reshape(D, GROUPS, HG, DV).transpose(1, 3, 2, 0).reshape(GROUPS, P, HG * D)
    w_groups = np.stack([grouped(arr("L0_attn_" + n)) for n in ("Wq", "Wk", "Wv", "Wg")] + [wo], axis=1)
    ws1 = np.zeros((P, KT, 4, 32), np.float32)
    ws1[:, :, :, :RANK] = arr("L0_attn_Ws1").reshape(RANK, KT, P).transpose(2, 1, 0)[:, :, None, :]
    ws2 = np.zeros((4, 32, HEADS * M), np.float32)
    ws2[:, :RANK] = arr("L0_attn_Ws2").T
    ws2[0::2, RANK] = arr("L0_attn_bs2")
    pos = np.arange(T, dtype=np.float32)
    inv_freq = (np.float32(1.0) / np.float32(10000.0) ** (np.arange(0, DK, 2, dtype=np.float32) / np.float32(DK)))
    ang = (pos[:, None] * inv_freq[None, :].astype(np.float32)).astype(np.float32)
    cos, sin = np.cos(ang).astype(np.float32), np.sin(ang).astype(np.float32)
    rope_cos = cos.reshape(CB, P, 64).transpose(1, 0, 2).reshape(P, CB * 64)
    rope_sin = np.concatenate([-sin, sin], axis=1).reshape(CB, P, 128).transpose(1, 0, 2).reshape(P, CB * 128)
    at = np.arange(P)
    keep_mask = (at[:, None] <= at[None, :]).astype(np.float32)
    arrays = {
        "hs_cols": hs_cols,
        "hs_rows": hs,
        "w_groups": w_groups,
        "ws1": ws1.reshape(P, KT * P),
        "ws2": ws2.reshape(P, HEADS * M),
        "gnorm": arr("L0_attn_g_norm_weight").reshape(P, 1),
        "ffn_w": arr("L0_ffn_weight").reshape(D, KT, P).transpose(2, 1, 0).reshape(P, KT * D),
        "ffn_scale": arr("L0_ffn_scale_weight"),
        "ffn_bias": arr("L0_ffn_bias"),
        "rope_cos": rope_cos,
        "rope_sin": rope_sin,
        "keep_mask": keep_mask,
        "below_mask": 1 - keep_mask,
        "identity": np.eye(P, dtype=np.float32),
    }
    arrays = {n: np.ascontiguousarray(a) for n, a in arrays.items()}
    nc = bacc.Bacc("TRN2", target_bir_lowering=False, num_devices=1)
    args = [nc.dram_tensor(n, a.shape, mybir.dt.from_np(a.dtype), kind="ExternalInput").ap() for n, a in arrays.items()]
    out = nc.dram_tensor("out", (CHUNKS, P, D), F32, kind="ExternalOutput").ap()
    gated_slot_attention_block(nc, *args, out)
    result = run_bass_kernel_spmd(nc, [arrays], core_ids=[0])
    return result.results[0]["out"].reshape(BATCH, T, D)
```

```python
from contextlib import ExitStack

import concourse.bass as bass
from concourse import mybir

P = 128
BATCH, T, D = 4, 512, 512
HEADS, DK, DV, M = 16, 128, 128, 64
RANK = 16
HG = 4
GROUPS = HEADS // HG
CB = T // P
CHUNKS = BATCH * CB
STEPS = GROUPS * CHUNKS
KT = D // P
F = HG * DK
H = HG * M
CLAMP, EPS = 32.0, 1e-5
SCALE = DK ** -0.5
WQ, WK, WV, WG, WO = range(5)

F32 = mybir.dt.float32
F32R = mybir.dt.float32r
ALU = mybir.AluOpType
ACT = mybir.ActivationFunctionType
AX = mybir.AxisListType


def gated_slot_attention_block(nc, hs_cols, hs_rows, w_groups, ws1, ws2, gnorm, ffn_w, ffn_scale, ffn_bias,
                               rope_cos, rope_sin, keep_mask, below_mask, identity, out):
    with ExitStack() as ctx:
        def sb(name, cols, dt=F32):
            return ctx.enter_context(nc.sbuf_tensor(name, [P, cols], dt))

        def bank(name):
            return ctx.enter_context(nc.psum_tensor(name, [P, 512], F32))

        def sem(name):
            return ctx.enter_context(nc.semaphore(name))

        u_dram = nc.dram_tensor("u_scratch", (CHUNKS, P, P), F32, kind="Internal").ap()
        part_dram = nc.dram_tensor("part_scratch", (1 + STEPS, P, D), F32, kind="Internal").ap()

        w_hi = [sb(f"w_hi{m}", KT * F, F32R) for m in range(4)]
        w_lo = [sb(f"w_lo{m}", KT * F, F32R) for m in range(4)]
        wo_hi, wo_lo = sb("wo_hi", HG * D, F32R), sb("wo_lo", HG * D, F32R)
        w_raw = [sb(f"w_raw{s}", KT * F) for s in range(2)]
        ws2_part = sb("ws2_part", HEADS * M, F32R)
        gn = sb("gn", 1)
        cos_t, sin_t = sb("cos_t", CB * 64), sb("sin_t", CB * 128)
        keep, ident = sb("keep", P), sb("ident", P)
        keep_r, below_r = sb("keep_r", P, F32R), sb("below_r", P, F32R)
        minus_half = sb("minus_half", HG)
        hs_raw = [sb(f"hs_raw{s}", KT * P) for s in range(2)]
        hs_hi = [sb(f"hs_hi{s}", KT * P, F32R) for s in range(2)]
        hs_lo = [sb(f"hs_lo{s}", KT * P, F32R) for s in range(2)]
        u_part = [sb(f"u_part{s}", P, F32R) for s in range(2)]
        rope_a, rope_b, q_rot = sb("rope_a", F), sb("rope_b", F), sb("q_rot", F)
        k_rot = [sb(f"k_rot{s}", F) for s in range(2)]
        qT, kT = sb("qT", F), sb("kT", F)
        v = [sb(f"v{s}", F) for s in range(2)]
        th = sb("th", F)
        gate = [sb(f"gate{s}", F) for s in range(2)]
        s_clip = sb("s_clip", H)
        es = [sb(f"es{s}", H) for s in range(2)]
        es_hi = [sb(f"es_hi{s}", H, F32R) for s in range(2)]
        es_lo = [sb(f"es_lo{s}", H, F32R) for s in range(2)]
        esT = sb("esT", H)
        enz = sb("enz", H)
        masked = sb("masked", F)
        ok, prob, slot_p = sb("ok", H), sb("prob", H), sb("slot_p", H)
        ok_max, p_sum, sum_sq = sb("ok_max", HG), sb("p_sum", HG), sb("sum_sq", HG)
        eps_sum, var, rms = sb("eps_sum", HG), sb("var", HG), sb("rms", HG)
        pT = sb("pT", F)
        s1, s2 = sb("s1", H), sb("s2", HG // 2 * DV)
        o_sq, o_gated, o_norm = sb("o_sq", F), sb("o_gated", F), sb("o_norm", F)
        oT_hi, oT_lo = sb("oT_hi", F, F32R), sb("oT_lo", F, F32R)
        part = [sb(f"part{s}", D) for s in range(2)]

        bank_qv, bank_kg, bank_t, bank_a, bank_s, bank_c, bank_s2, bank_o = [
            bank(n) for n in ("bank_qv", "bank_kg", "bank_t", "bank_a", "bank_s", "bank_c", "bank_s2", "bank_o")]
        cums, s1_acc = bank_c[:, 0:H], bank_c[:, H:2 * H]

        wf_hi, wf_lo, wf_raw, wf_scaled = w_hi[0], w_lo[0], w_raw[1], w_raw[0]
        scale_row, bias_row = rope_a, rope_b
        x_parts = [w_hi[2][:, :].bitcast(F32), w_lo[2][:, :].bitcast(F32)]
        sum_a, sum_b, x_row, y_row = th, q_rot, o_sq, [o_gated, o_norm]
        x1 = k_rot
        x1T_hi = [sb(f"x1T_hi{s}", D, F32R) for s in range(2)]
        x1T_lo = [sb(f"x1T_lo{s}", D, F32R) for s in range(2)]
        z = gate
        stats, mean_var, shifted_var, rstd = sb("stats", 6), sb("mean_var", 2), sb("shifted_var", 1), sb("rstd", 1)
        stats2, mean_var2, shifted_var2, rstd2 = (
            sb("stats2", 6), sb("mean_var2", 2), sb("shifted_var2", 1), sb("rstd2", 1))

        const_in, pre_in, batch_in = sem("const_in"), sem("pre_in"), sem("batch_in")
        stored = [sem(f"stored{s}") for s in range(2)]
        hs_in, u_in = [sem(f"hs_in{s}") for s in range(2)], [sem(f"u_in{s}") for s in range(2)]
        w_in = [sem(f"w_in{s}") for s in range(2)]
        zeroed, ones_set, consts_made, ws2_made = sem("zeroed"), sem("ones_set"), sem("consts_made"), sem("ws2_made")
        u_mm, u_hi_made, u_made = sem("u_mm"), sem("u_hi_made"), sem("u_made")
        hs_hi_made, hs_lo_made = sem("hs_hi_made"), sem("hs_lo_made")
        w_hi_made, w_lo_made, wo_hi_made, wo_lo_made = (
            sem("w_hi_made"), sem("w_lo_made"), sem("wo_hi_made"), sem("wo_lo_made"))
        q_mm, k_mm, v_mm, g_mm, s_mm, out_mm = [sem(n) for n in ("q_mm", "k_mm", "v_mm", "g_mm", "s_mm", "out_mm")]
        a_mm, ok_mm, w2_mm, o_mm, s1_mm, s2_mm, cums_mm = [
            sem(n) for n in ("a_mm", "ok_mm", "w2_mm", "o_mm", "s1_mm", "s2_mm", "cums_mm")]
        qT_mm, kT_mm, pT_mm, esT_mm, oT_mm = [sem(n) for n in ("qT_mm", "kT_mm", "pT_mm", "esT_mm", "oT_mm")]
        q_turned, q_summed, k_turned, k_summed = [sem(n) for n in ("q_turned", "q_summed", "k_turned", "k_summed")]
        qT_made, kT_made, v_made, s1_made, s2_made, a_masked, w2_masked = [
            sem(n) for n in ("qT_made", "kT_made", "v_made", "s1_made", "s2_made", "a_masked", "w2_masked")]
        th_made, gate_made, s_clipped, es_made, es_hi_made, es_lo_made, esT_made, enz_made = [
            sem(n) for n in ("th_made", "gate_made", "s_clipped", "es_made", "es_hi_made", "es_lo_made",
                             "esT_made", "enz_made")]
        ok_scaled, ok_maxed, ok_shifted, prob_made, prob_summed, slot_p_made, pT_made = [
            sem(n) for n in ("ok_scaled", "ok_maxed", "ok_shifted", "prob_made", "prob_summed", "slot_p_made",
                             "pT_made")]
        o_squared, sq_summed, eps_scaled, var_made, rms_made, o_gated_made, o_norm_made = [
            sem(n) for n in ("o_squared", "sq_summed", "eps_scaled", "var_made", "rms_made", "o_gated_made",
                             "o_norm_made")]
        oT_hi_made, oT_lo_made, part_made = sem("oT_hi_made"), sem("oT_lo_made"), sem("part_made")
        wf_in, row_in, wf_scaled_made, wf_hi_made, wf_lo_made = [
            sem(n) for n in ("wf_in", "row_in", "wf_scaled_made", "wf_hi_made", "wf_lo_made")]
        x_in = [sem(f"x_in{s}") for s in range(2)]
        sum_a_made, sum_b_made, sum_c_made, x_made, stats_made, mean_made, shifted_made, rstd_made, x1_made = [
            sem(n) for n in ("sum_a_made", "sum_b_made", "sum_c_made", "x_made", "stats_made", "mean_made",
                             "shifted_made", "rstd_made", "x1_made")]
        biased_made, x1T_mm, x1T_hi_made, x1T_lo_made, ffn_mm, y_made = [
            sem(n) for n in ("biased_made", "x1T_mm", "x1T_hi_made", "x1T_lo_made", "ffn_mm", "y_made")]
        stats2_made, mean2_made, shifted2_made, rstd2_made, z_made = [
            sem(n) for n in ("stats2_made", "mean2_made", "shifted2_made", "rstd2_made", "z_made")]

        U_STORES = BATCH // 2
        LOOP_STORES = [U_STORES + STEPS // 2 + 1, U_STORES + STEPS // 2]

        def done(u, c, ahead=0):
            return u * CB + (c + 1 + ahead)

        def carried(u, c):
            return u * (CB - 1) + (c + 1)

        def all_steps(eng, body):
            with eng.Fori(0, GROUPS) as g:
                with eng.Fori(0, BATCH - 1) as b:
                    for c in range(CB):
                        body(g * BATCH + b, g, b, c, False)
                for c in range(CB):
                    body(g * BATCH + (BATCH - 1), g, BATCH - 1, c, True)

        SLOT = {WQ: 1, WK: 0, WV: 1, WG: 0, WO: 0}

        def raw_in(m, g, b=0):
            if m == WO:
                return g * 6 + b + 3
            return (g * 6 + (1 if m == WK else 2)) if SLOT[m] == 0 else (g * 2 + (1 if m == WQ else 2))

        def per_head(ap, n=HG):
            return ap.rearrange("p (h x) -> p h x", h=n)

        def over_heads(ap, n=HG):
            return ap.unsqueeze(1).broadcast_to([P, n, ap.shape[1]])

        def over_columns(ap, n):
            return ap.unsqueeze(2).broadcast_to([P, ap.shape[1], n])

        def of_pair(ap, half, n):
            return ap[64 * half:64 * half + 64, :].rearrange("p (r e x) -> p r e x", e=2, x=n)[:, :, half, :]

        def x_loads(j, s):
            return (j - s) * (5 * 16 // 2) + 5 * 16

        def last_phase(eng, front, back):
            front(0, 0)
            with eng.Fori(0, CHUNKS // 2 - 1) as jj:
                for s in range(2):
                    front(jj * 2 + (s + 1), 1 - s)
                    back(jj * 2 + s, s)
            front(CHUNKS - 1, 1)
            back(CHUNKS - 2, 0)
            back(CHUNKS - 1, 1)

        block = ctx.enter_context(nc.Block())

        @block.sync
        def _(sp):
            for dst, src in ((cos_t, rope_cos), (sin_t, rope_sin), (keep, keep_mask), (ident, identity), (gn, gnorm)):
                sp.dma_start(dst[:, :], src).then_inc(const_in, 16)
            sp.dma_start(w_raw[0][:, 0:KT * P], ws1).then_inc(pre_in, 16)
            sp.dma_start(w_raw[0][:, KT * P:KT * P + P], below_mask).then_inc(pre_in, 16)
            sp.dma_start(w_raw[0][:, 1024:2048], ws2).then_inc(pre_in, 16)
            for b in range(BATCH):
                if b:
                    sp.wait_ge(u_mm, b)
                for c in range(CB):
                    sp.dma_start(w_raw[1][:, :].rearrange("p (k c t) -> p k c t", k=KT, c=CB)[:, :, c, :],
                                 hs_cols[CB * b + c].rearrange("p (k t) -> p k t", k=KT)).then_inc(batch_in, 16)
                sp.wait_ge(u_made, b + 1)
                sp.dma_start(u_dram[CB * b:CB * b + CB].rearrange("c p t -> p c t"),
                             part[b % 2][:, :].rearrange("p (c t) -> p c t", c=CB)).then_inc(stored[b % 2], 16)
            for s in range(2):
                sp.wait_ge(stored[s], 16 * U_STORES)
            sp.wait_ge(ws2_made, 3)
            sp.wait_ge(consts_made, 2)

            def load_hs(slot, chunk):
                sp.dma_start(hs_raw[slot][:, :], hs_cols[chunk]).then_inc(hs_in[slot], 16)

            def load_u(slot, chunk):
                sp.dma_start(u_part[slot][:, :].bitcast(F32), u_dram[chunk]).then_inc(u_in[slot], 16)

            def load_w(m, g):
                sp.dma_start(w_raw[SLOT[m]][:, :], w_groups[g, m]).then_inc(w_in[SLOT[m]], 16)

            def w_split(count):
                sp.wait_ge(w_hi_made, count)
                sp.wait_ge(w_lo_made, count)

            for i in range(2):
                load_hs(i, i)
                load_u(i, i)
            load_w(WQ, 0)
            load_w(WK, 0)
            w_split(1)
            load_w(WV, 0)
            w_split(2)
            load_w(WG, 0)
            w_split(4)
            load_w(WO, 0)

            def step(u, g, b, c, last):
                chunk = c - 2 if last and c >= 2 else b * CB + (c + 2)
                sp.wait_ge(hs_hi_made, done(u, c))
                sp.wait_ge(hs_lo_made, done(u, c))
                load_hs(c % 2, chunk)
                sp.wait_ge(s_mm, done(u, c))
                load_u(c % 2, chunk)
                if c == 1:
                    sp.wait_ge(wo_hi_made, u + 1)
                    sp.wait_ge(wo_lo_made, u + 1)
                    if last:
                        load_w(WQ, (g + 1) % GROUPS)
                        load_w(WK, (g + 1) % GROUPS)
                    else:
                        load_w(WO, g)
                if c == 2 and last:
                    w_split(g * 4 + 5)
                    load_w(WV, (g + 1) % GROUPS)
                    w_split(g * 4 + 6)
                    load_w(WG, (g + 1) % GROUPS)
                sp.wait_ge(part_made, done(u, c))
                sp.dma_start(part_dram[u * CB + c], part[c % 2][:, :]).then_inc(stored[c % 2], 16)
                if c == 3 and last:
                    w_split(g * 4 + 8)
                    load_w(WO, (g + 1) % GROUPS)

            all_steps(sp, step)
            sp.wait_ge(part_made, STEPS + 1)
            sp.dma_start(part_dram[STEPS], part[0][:, :]).then_inc(stored[0], 16)
            sp.wait_ge(w_in[0], 16 * raw_in(WO, GROUPS))
            sp.wait_ge(o_norm_made, STEPS + 1)
            sp.wait_ge(gate_made, STEPS + 1)
            sp.dma_start(wf_raw[:, :], ffn_w).then_inc(wf_in, 16)
            sp.dma_start(scale_row[:, :], ffn_scale.partition_broadcast(P)).then_inc(row_in, 16)
            sp.dma_start(bias_row[:, :], ffn_bias.partition_broadcast(P)).then_inc(row_in, 16)
            sp.wait_ge(stored[0], 16 * LOOP_STORES[0])
            sp.wait_ge(stored[1], 16 * LOOP_STORES[1])
            sp.wait_ge(hs_hi_made, STEPS + 1)
            sp.wait_ge(hs_lo_made, STEPS + 1)

            def load_x(j, slot):
                sp.dma_start(hs_raw[slot][:, :], hs_rows[j]).then_inc(x_in[slot], 16)
                for g in range(GROUPS):
                    sp.dma_start(x_parts[slot][:, D * g:D * g + D], part_dram[j + (1 + g * CHUNKS)]
                                 ).then_inc(x_in[slot], 16)

            for s in range(2):
                sp.wait_ge(hs_in[s], 16 * (STEPS // 2 + 1))
                sp.wait_ge(u_in[s], 16 * (STEPS // 2 + 1))
                load_x(s, s)

            def row(j, s, more):
                if more:
                    sp.wait_ge(x_made, j + 1)
                    load_x(j + 2, s)
                sp.wait_ge(z_made, j + 1)
                sp.dma_start(out[j], z[s][:, :]).then_inc(stored[s], 16)

            with sp.Fori(0, CHUNKS // 2 - 1) as jj:
                for s in range(2):
                    row(jj * 2 + s, s, True)
            for s in range(2):
                row(CHUNKS - 2 + s, s, False)
            for s in range(2):
                sp.wait_ge(stored[s], 16 * (LOOP_STORES[s] + CHUNKS // 2))

        @block.gpsimd
        def _(pool):
            for t, value in ((part[0], 1.0), (part[1], 1.0)):
                pool.memset(t[:, :], value).then_inc(ones_set, 1)
            pool.memset(pT[:, :], 0.0).then_inc(zeroed, 1)
            for t in (wo_hi, wo_lo):
                pool.memset(t[:, :].bitcast(F32), 0.0).then_inc(zeroed, 1)
            pool.memset(o_gated[:, :], 0.0).then_inc(o_gated_made, 1)
            pool.memset(var[:, :], 1.0).then_inc(var_made, 1)
            pool.memset(minus_half[:, :], -0.5).then_inc(zeroed, 1)

            def hs_split(slot, n):
                pool.wait_ge(hs_hi_made, n)
                pool.tensor_tensor(hs_lo[slot][:, :], hs_raw[slot][:, :], hs_hi[slot][:, :].bitcast(F32),
                                   ALU.subtract).then_inc(hs_lo_made, 1)

            def q_sum(n):
                pool.wait_ge(q_turned, n)
                pool.tensor_tensor(q_rot[:, :], rope_a[:, :], rope_b[:, :], ALU.add).then_inc(q_summed, 1)

            def k_sum(slot, n):
                pool.wait_ge(k_turned, n)
                pool.tensor_tensor(k_rot[slot][:, :], rope_a[:, :], rope_b[:, :], ALU.add).then_inc(k_summed, 1)

            def es_split(slot, n):
                pool.wait_ge(es_hi_made, n)
                pool.tensor_tensor(es_lo[slot][:, :], es[slot][:, :], es_hi[slot][:, :].bitcast(F32),
                                   ALU.subtract).then_inc(es_lo_made, 1)

            hs_split(0, 1)
            q_sum(1)
            k_sum(0, 1)
            es_split(0, 1)
            hs_split(1, 2)
            pool.wait_ge(zeroed, 4)

            def step(u, g, b, c, last):
                pool.wait_ge(o_gated_made, done(u, c))
                pool.wait_ge(var_made, done(u, c))
                pool.tensor_tensor(rms[:, :], var[:, :], minus_half[:, :], ALU.pow).then_inc(rms_made, 1)
                pool.wait_ge(rms_made, done(u, c))
                pool.tensor_tensor(per_head(o_norm[:, :]), per_head(o_gated[:, :]), over_columns(rms[:, :], DV),
                                   ALU.mult).then_inc(o_norm_made, 1)
                q_sum(done(u, c, 1))
                pool.wait_ge(ok_maxed, done(u, c))
                pool.tensor_tensor(per_head(ok[:, :]), per_head(ok[:, :]), over_columns(ok_max[:, :], M),
                                   ALU.subtract).then_inc(ok_shifted, 1)
                pool.wait_ge(prob_made, done(u, c))
                pool.tensor_tensor(slot_p[:, :], prob[:, :], enz[:, :], ALU.mult).then_inc(slot_p_made, 1)
                k_sum((c + 1) % 2, done(u, c, 1))
                es_split((c + 1) % 2, done(u, c, 1))
                hs_split(c % 2, done(u, c, 2))

            all_steps(pool, step)
            pool.wait_ge(o_gated_made, STEPS + 1)
            pool.wait_ge(var_made, STEPS + 1)
            pool.tensor_tensor(rms[:, :], var[:, :], minus_half[:, :], ALU.pow).then_inc(rms_made, 1)
            pool.wait_ge(rms_made, STEPS + 1)
            pool.tensor_tensor(per_head(o_norm[:, :]), per_head(o_gated[:, :]), over_columns(rms[:, :], DV),
                               ALU.mult).then_inc(o_norm_made, 1)

            def front(j, s):
                if not (isinstance(j, int) and j == 0):
                    pool.wait_ge(x_made, j)
                pool.wait_ge(x_in[s], x_loads(j, s))
                pool.tensor_tensor(sum_a[:, :], x_parts[s][:, 0:D], x_parts[s][:, D:2 * D], ALU.add
                                   ).then_inc(sum_a_made, 1)
                pool.wait_ge(shifted_made, j + 1)
                pool.tensor_tensor(rstd[:, :], shifted_var[:, :], minus_half[:, 0:1], ALU.pow).then_inc(rstd_made, 1)
                pool.wait_ge(x1_made, j + 1)
                pool.wait_ge(row_in, 32)
                pool.wait_ge(x1T_mm, j + 1)
                pool.tensor_tensor(x1[s][:, :], x1[s][:, :], bias_row[:, :], ALU.add).then_inc(biased_made, 1)

            def back(j, s):
                pool.wait_ge(shifted2_made, j + 1)
                pool.tensor_tensor(rstd2[:, :], shifted_var2[:, :], minus_half[:, 0:1], ALU.pow
                                   ).then_inc(rstd2_made, 1)

            last_phase(pool, front, back)

        @block.scalar
        def _(act):
            def copy(dst, src, scale=1.0):
                return act.activation(dst, src, ACT.Copy, scale=scale)

            act.wait_ge(const_in, 16 * 5)
            copy(keep_r[:, :], keep[:, :]).then_inc(consts_made, 1)
            act.wait_ge(pre_in, 16 * 3)
            copy(below_r[:, :], w_raw[0][:, KT * P:KT * P + P]).then_inc(consts_made, 1)
            copy(ws2_part[0:64, :], w_raw[0][0:64, 1024:2048]).then_inc(ws2_made, 1)
            copy(w_hi[0][64:128, 0:1024], w_raw[0][64:128, 1024:2048]).then_inc(ws2_made, 1)
            act.wait_ge(ones_set, 2)
            for b in range(BATCH):
                act.wait_ge(u_mm, b + 1)
                if b >= 2:
                    act.wait_ge(stored[b % 2], 16 * (b // 2))
                if b:
                    act.wait_ge(u_made, b)
                copy(rope_a[:, :].bitcast(F32R), bank_qv[:, :])
                copy(part[b % 2][0:RANK, :].bitcast(F32R), bank_qv[0:RANK, :])
                copy(part[b % 2][64:64 + RANK, :].bitcast(F32R), bank_qv[64:64 + RANK, :]).then_inc(u_hi_made, 1)

            def w_split(m, loads):
                act.wait_ge(w_in[SLOT[m]], 16 * loads)
                copy(w_hi[m][:, :], w_raw[SLOT[m]][:, :]).then_inc(w_hi_made, 1)

            def hs_split(slot, n_in):
                act.wait_ge(hs_in[slot], n_in)
                copy(hs_hi[slot][:, :], hs_raw[slot][:, :]).then_inc(hs_hi_made, 1)

            def exp_s(slot, n):
                act.wait_ge(s_clipped, n)
                act.activation(es[slot][:, :], s_clip[:, :], ACT.Exp).then_inc(es_made, 1)
                act.wait_ge(es_made, n)
                copy(es_hi[slot][:, :], es[slot][:, :]).then_inc(es_hi_made, 1)

            def from_bank(dst, src, wait, n, made):
                act.wait_ge(wait, n)
                copy(dst, src).then_inc(made, 1)

            hs_split(0, 16)
            act.wait_ge(ws2_made, 3)
            for m in (WQ, WK, WV, WG):
                w_split(m, raw_in(m, 0))
            act.wait_ge(zeroed, 4)
            from_bank(qT[:, :], bank_t[:, :], qT_mm, 1, qT_made)
            exp_s(0, 1)
            from_bank(v[0][:, :], bank_qv[:, :], v_mm, 1, v_made)
            from_bank(esT[:, :], bank_t[:, 0:H], esT_mm, 1, esT_made)
            act.wait_ge(g_mm, 1)
            act.activation(th[:, :], bank_kg[:, :], ACT.Tanh, scale=0.5).then_inc(th_made, 1)
            from_bank(kT[:, :], bank_t[:, :], kT_mm, 1, kT_made)
            hs_split(1, 16)

            def step(u, g, b, c, last):
                i, n = done(u, c), done(u, c, 1)
                act.wait_ge(ok_shifted, i)
                act.activation(prob[:, :], ok[:, :], ACT.Exp).then_inc(prob_made, 1)
                if last and c == 2:
                    act.wait_ge(q_mm, n)
                    w_split(WQ, g * 2 + 3)
                from_bank(qT[:, :], bank_t[:, :], qT_mm, n, qT_made)
                from_bank(oT_hi[:, :], bank_t[:, :], oT_mm, i, oT_hi_made)
                exp_s((c + 1) % 2, n)
                if last and c == 2:
                    act.wait_ge(k_mm, n)
                    w_split(WK, g * 6 + 7)
                from_bank(v[(c + 1) % 2][:, :], bank_qv[:, :], v_mm, n, v_made)
                act.wait_ge(pT_mm, i)
                copy(of_pair(pT[:, :], 0, P), per_head(bank_t[0:64, 0:H], 2))
                copy(of_pair(pT[:, :], 1, P), per_head(bank_t[64:128, 0:H], 2)).then_inc(pT_made, 1)
                if last and c == 2:
                    w_split(WV, g * 2 + 4)
                act.wait_ge(out_mm, i)
                act.wait_ge(stored[c % 2], (u * (CB // 2) + (c // 2 + U_STORES)) * 16)
                copy(part[c % 2][:, :], bank_o[:, :]).then_inc(part_made, 1)
                if c == 0:
                    act.wait_ge(w_in[0], (g * 6 + b + 3) * 16)
                    copy(wo_hi[:, :], w_raw[0][:, :], gn[:, 0:1]).then_inc(wo_hi_made, 1)
                from_bank(esT[:, :], bank_t[:, 0:H], esT_mm, n, esT_made)
                act.wait_ge(g_mm, n)
                act.activation(th[:, :], bank_kg[:, :], ACT.Tanh, scale=0.5).then_inc(th_made, 1)
                from_bank(kT[:, :], bank_t[:, :], kT_mm, n, kT_made)
                hs_split(c % 2, (u * (CB // 2) + (c // 2 + 2)) * 16)
                if last and c == 2:
                    w_split(WG, g * 6 + 8)
                act.wait_ge(o_mm, i)
                act.activation(o_sq[:, :], bank_o[:, :], ACT.Square).then_inc(o_squared, 1)
                if c < CB - 1:
                    from_bank(s1[:, :], s1_acc, s1_mm, carried(u, c), s1_made)
                    act.wait_ge(s2_mm, carried(u, c))
                    copy(per_head(s2[0:64, :], 2), of_pair(bank_s2[:, :], 0, DV))
                    copy(per_head(s2[64:128, :], 2), of_pair(bank_s2[:, :], 1, DV)).then_inc(s2_made, 1)

            all_steps(act, step)
            from_bank(oT_hi[:, :], bank_t[:, :], oT_mm, STEPS + 1, oT_hi_made)
            act.wait_ge(out_mm, STEPS + 1)
            act.wait_ge(stored[0], (STEPS // 2 + U_STORES) * 16)
            copy(part[0][:, :], bank_o[:, :]).then_inc(part_made, 1)

            act.wait_ge(wf_scaled_made, KT)
            copy(wf_hi[:, :], wf_scaled[:, :]).then_inc(wf_hi_made, 1)

            def front(j, s):
                act.wait_ge(x1T_mm, j + 1)
                copy(x1T_hi[s][:, :], bank_t[:, :]).then_inc(x1T_hi_made, 1)

            last_phase(act, front, lambda j, s: None)

        @block.vector
        def _(dve):
            def minus_hi(dst, src, hi):
                return dve.tensor_tensor(dst, src, hi.bitcast(F32), ALU.subtract)

            dve.wait_ge(ws2_made, 2)
            minus_hi(ws2_part[64:128, :], w_raw[0][64:128, 1024:2048], w_hi[0][64:128, 0:1024]).then_inc(ws2_made, 1)
            for b in range(BATCH):
                dve.wait_ge(u_hi_made, b + 1)
                for q in (32, 96):
                    last = minus_hi(part[b % 2][q:q + RANK, :].bitcast(F32R), bank_qv[q:q + RANK, :],
                                    rope_a[q:q + RANK, :])
                last.then_inc(u_made, 1)

            def rotate(chunk, bank_in, turned, n):
                halves = "p (r x) -> p r x"
                x = bank_in[:, :].rearrange(halves, x=DK // 2)
                dve.tensor_tensor(rope_a[:, :].rearrange(halves, x=DK // 2), x,
                                  over_heads(cos_t[:, 64 * chunk:64 * chunk + 64], 2 * HG), ALU.mult)
                sins = sin_t[:, 128 * chunk:128 * chunk + 128]
                for half in range(2):
                    x = bank_in[:, :].rearrange("p (h e x) -> p h e x", e=2, x=DK // 2)[:, :, 1 - half, :]
                    y = rope_b[:, :].rearrange("p (h e x) -> p h e x", e=2, x=DK // 2)[:, :, half, :]
                    last = dve.tensor_tensor(y, x, over_heads(sins[:, 64 * half:64 * half + 64]), ALU.mult)
                last.then_inc(turned, 1)

            def rotate_q(chunk, n, first=False):
                dve.wait_ge(q_mm, n)
                if not first:
                    dve.wait_ge(k_summed, n - 1)
                rotate(chunk, bank_qv, q_turned, n)

            def rotate_k(chunk, n):
                dve.wait_ge(k_mm, n)
                dve.wait_ge(q_summed, n)
                rotate(chunk, bank_kg, k_turned, n)

            def w_split(m, n):
                dve.wait_ge(w_hi_made, n)
                minus_hi(w_lo[m][:, :], w_raw[SLOT[m]][:, :], w_hi[m][:, :]).then_inc(w_lo_made, 1)

            def lo(dst, src, hi, hi_made, n, made):
                dve.wait_ge(hi_made, n)
                minus_hi(dst, src, hi).then_inc(made, 1)

            def clip(n):
                dve.wait_ge(s_mm, n)
                dve.tensor_scalar(s_clip[:, :], bank_s[:, 0:H], CLAMP, -CLAMP, ALU.min, ALU.max).then_inc(s_clipped, 1)

            def make_gate(slot, n):
                dve.wait_ge(th_made, n)
                dve.scalar_tensor_tensor(gate[slot][:, :], th[:, :], 1.0, bank_kg[:, :], ALU.add, ALU.mult
                                         ).then_inc(gate_made, 1)

            def make_enz(n):
                dve.wait_ge(cums_mm, n)
                dve.reciprocal(enz[:, :], cums).then_inc(enz_made, 1)

            def mask(mm, n, made):
                dve.wait_ge(mm, n)
                dve.tensor_tensor(per_head(masked[:, :]), per_head(bank_a[:, :]), over_heads(keep[:, :]), ALU.mult
                                  ).then_inc(made, 1)

            dve.wait_ge(const_in, 16 * 5)
            for m in (WQ, WK, WV, WG):
                w_split(m, m + 1)
            rotate_q(0, 1, first=True)
            rotate_k(0, 1)
            clip(1)
            make_gate(0, 1)
            make_enz(1)
            mask(a_mm, 1, a_masked)
            dve.wait_ge(zeroed, 4)

            def step(u, g, b, c, last):
                i, n = done(u, c), done(u, c, 1)
                rotate_q((c + 1) % CB, n)
                dve.wait_ge(ok_mm, i)
                dve.scalar_tensor_tensor(ok[:, :], bank_s[:, 0:H], SCALE, enz[:, :], ALU.mult, ALU.mult
                                         ).then_inc(ok_scaled, 1)
                dve.wait_ge(ok_scaled, i)
                dve.tensor_reduce(ok_max[:, :], per_head(ok[:, :]), AX.X, ALU.max).then_inc(ok_maxed, 1)
                dve.wait_ge(prob_made, i)
                dve.tensor_reduce(p_sum[:, :], per_head(prob[:, :]), AX.X, ALU.add).then_inc(prob_summed, 1)
                if last and c == 2:
                    w_split(WQ, g * 4 + 5)
                rotate_k((c + 1) % CB, n)
                clip(n)
                lo(oT_lo[:, :], bank_t[:, :], oT_hi[:, :], oT_hi_made, i, oT_lo_made)
                if last and c == 2:
                    w_split(WK, g * 4 + 6)
                dve.wait_ge(prob_summed, i)
                dve.scalar_tensor_tensor(eps_sum[:, :], p_sum[:, :], 4 * EPS, p_sum[:, :], ALU.mult, ALU.mult
                                         ).then_inc(eps_scaled, 1)
                if last and c == 2:
                    w_split(WV, g * 4 + 7)
                if c == 0:
                    dve.wait_ge(wo_hi_made, u + 1)
                    dve.scalar_tensor_tensor(wo_lo[:, :], w_raw[0][:, :], gn[:, 0:1], wo_hi[:, :].bitcast(F32),
                                             ALU.mult, ALU.subtract).then_inc(wo_lo_made, 1)
                mask(w2_mm, i, w2_masked)
                make_gate((c + 1) % 2, n)
                make_enz(n)
                if last and c == 2:
                    w_split(WG, g * 4 + 8)
                dve.wait_ge(o_squared, i)
                dve.wait_ge(o_norm_made, i)
                dve.tensor_tensor(o_gated[:, :], bank_o[:, :], gate[c % 2][:, :], ALU.mult).then_inc(o_gated_made, 1)
                dve.tensor_reduce(sum_sq[:, :], per_head(o_sq[:, :]), AX.X, ALU.add).then_inc(sq_summed, 1)
                dve.wait_ge(sq_summed, i)
                dve.wait_ge(eps_scaled, i)
                dve.scalar_tensor_tensor(var[:, :], sum_sq[:, :], 4.0 / DV, eps_sum[:, :], ALU.mult, ALU.add
                                         ).then_inc(var_made, 1)
                mask(a_mm, n, a_masked)

            all_steps(dve, step)
            lo(oT_lo[:, :], bank_t[:, :], oT_hi[:, :], oT_hi_made, STEPS + 1, oT_lo_made)

            dve.wait_ge(wf_in, 16)
            dve.wait_ge(row_in, 32)
            for k in range(KT):
                cols = slice(D * k, D * k + D)
                dve.tensor_tensor(wf_scaled[:, cols], wf_raw[:, cols], scale_row[:, :], ALU.mult
                                  ).then_inc(wf_scaled_made, 1)
            dve.wait_ge(wf_hi_made, 1)
            minus_hi(wf_lo[:, :], wf_scaled[:, :], wf_hi[:, :]).then_inc(wf_lo_made, 1)

            def norm(x, dst, j, st, mv, sh, rs, made, m_stats, m_mean, m_shift, m_rstd, m_dst):
                dve.wait_ge(made, j + 1)
                dve.bn_stats(st[:, :], x).then_inc(m_stats, 1)
                dve.wait_ge(const_in, 16 * 5)
                dve.wait_ge(m_stats, j + 1)
                dve.bn_aggr(mv[:, :], st[:, :]).then_inc(m_mean, 1)
                dve.wait_ge(m_mean, j + 1)
                dve.tensor_scalar(sh[:, :], mv[:, 1:2], EPS, None, ALU.add).then_inc(m_shift, 1)
                dve.wait_ge(m_rstd, j + 1)
                dve.tensor_scalar(dst, x, mv[:, 0:1], rs[:, 0:1], ALU.subtract, ALU.mult).then_inc(m_dst, 1)

            def front(j, s):
                dve.wait_ge(x_in[s], x_loads(j, s))
                dve.tensor_tensor(sum_b[:, :], x_parts[s][:, 2 * D:3 * D], x_parts[s][:, 3 * D:4 * D], ALU.add
                                  ).then_inc(sum_b_made, 1)
                dve.wait_ge(sum_b_made, j + 1)
                dve.tensor_tensor(x_row[:, :], sum_b[:, :], hs_raw[s][:, :], ALU.add).then_inc(sum_c_made, 1)
                dve.wait_ge(sum_c_made, j + 1)
                dve.wait_ge(sum_a_made, j + 1)
                dve.tensor_tensor(x_row[:, :], x_row[:, :], sum_a[:, :], ALU.add).then_inc(x_made, 1)
                norm(x_row[:, :], x1[s][:, :], j, stats, mean_var, shifted_var, rstd, x_made, stats_made, mean_made,
                     shifted_made, rstd_made, x1_made)
                lo(x1T_lo[s][:, :], bank_t[:, :], x1T_hi[s][:, :], x1T_hi_made, j + 1, x1T_lo_made)

            def back(j, s):
                dve.wait_ge(ffn_mm, j + 1)
                dve.wait_ge(biased_made, j + 1)
                dve.tensor_tensor(y_row[s][:, :], bank_o[:, :], x1[s][:, :], ALU.add).then_inc(y_made, 1)
                dve.wait_ge(stored[s], (j - s) * (16 // 2) + 16 * LOOP_STORES[s])
                norm(y_row[s][:, :], z[s][:, :], j, stats2, mean_var2, shifted_var2, rstd2, y_made, stats2_made,
                     mean2_made, shifted2_made, rstd2_made, z_made)

            last_phase(dve, front, back)

        @block.tensor
        def _(pe):
            def product(dst, lhs, rhs, start=True, stop=True, **kw):
                for n, (x, y) in enumerate(((lhs[0], rhs[0]), (lhs[0], rhs[1]), (lhs[1], rhs[0]))):
                    mm = pe.matmul(dst, x, y, start=start and n == 0, stop=stop and n == 2, **kw)
                return mm

            def cols(pair, a, n):
                return tuple(t[:, a:a + n] for t in pair)

            def project(m, dst, slot):
                for k in range(KT):
                    mm = product(dst[:, :], cols((hs_hi[slot], hs_lo[slot]), P * k, P),
                                 cols((w_hi[m], w_lo[m]), F * k, F), start=k == 0, stop=k == KT - 1)
                return mm

            def transposes(src, n=HG):
                for h in range(n):
                    mm = pe.transpose(bank_t[:, P * h:P * h + P], src[:, P * h:P * h + P], ident[:, :])
                return mm

            def w_ready(n):
                pe.wait_ge(w_hi_made, n)
                pe.wait_ge(w_lo_made, n)

            def running_sum(slot, n, first):
                pe.wait_ge(es_hi_made, n)
                pe.wait_ge(es_lo_made, n)
                if not first:
                    for t in (es_hi, es_lo):
                        pe.matmul(cums, below_r[:, :], t[1 - slot][:, :], start=False, stop=False,
                                  skip_group_check=True)
                pe.matmul(cums, keep_r[:, :], es_hi[slot][:, :], start=first, stop=False, skip_group_check=True)
                pe.matmul(cums, keep_r[:, :], es_lo[slot][:, :], start=False, stop=True, skip_group_check=True
                          ).then_inc(cums_mm, 1)

            def scores(n):
                pe.wait_ge(kT_made, n)
                for h in range(HG):
                    mm = pe.matmul(bank_a[:, P * h:P * h + P], kT[:, P * h:P * h + P], qT[:, P * h:P * h + P],
                                   start=True, stop=True)
                mm.then_inc(a_mm, 1)

            pe.wait_ge(const_in, 16 * 5)
            pe.wait_ge(pre_in, 16 * 3)
            for b in range(BATCH):
                pe.wait_ge(batch_in, 16 * CB * (b + 1))
                if b:
                    pe.wait_ge(u_made, b)
                for k in range(KT):
                    mm = pe.matmul(bank_qv[:, :], w_raw[0][:, P * k:P * k + P], w_raw[1][:, T * k:T * k + T],
                                   start=k == 0, stop=k == KT - 1)
                mm.then_inc(u_mm, 1)
            pe.wait_ge(u_made, BATCH)
            pe.wait_ge(consts_made, 2)
            pe.wait_ge(hs_hi_made, 1)
            pe.wait_ge(hs_lo_made, 1)
            w_ready(1)
            project(WQ, bank_qv, 0).then_inc(q_mm, 1)
            w_ready(2)
            project(WK, bank_kg, 0).then_inc(k_mm, 1)
            pe.wait_ge(q_summed, 1)
            transposes(q_rot).then_inc(qT_mm, 1)
            pe.wait_ge(u_in[0], 16)
            pe.matmul(bank_s[:, 0:H], u_part[0][:, :], ws2_part[:, 0:H], start=True, stop=True).then_inc(s_mm, 1)
            w_ready(3)
            project(WV, bank_qv, 0).then_inc(v_mm, 1)
            pe.wait_ge(qT_made, 1)
            pe.wait_ge(es_made, 1)
            transposes(es[0], HG // 2).then_inc(esT_mm, 1)
            w_ready(4)
            pe.wait_ge(k_turned, 1)
            project(WG, bank_kg, 0).then_inc(g_mm, 1)
            pe.wait_ge(k_summed, 1)
            pe.wait_ge(esT_made, 1)
            transposes(k_rot[0]).then_inc(kT_mm, 1)
            running_sum(0, 1, True)
            scores(1)

            def step(u, g, b, c, last):
                i, n = done(u, c), done(u, c, 1)
                now, nxt = c % 2, (c + 1) % 2
                w_set = (g * 4 + 8) if last and c == CB - 1 else g * 4 + 4
                pe.wait_ge(hs_hi_made, n)
                pe.wait_ge(hs_lo_made, n)
                pe.wait_ge(v_made, i)
                if last and c == CB - 1:
                    w_ready(g * 4 + 5)
                project(WQ, bank_qv, nxt).then_inc(q_mm, 1)
                pe.wait_ge(a_masked, i)
                if c:
                    pe.wait_ge(s1_made, carried(u, c - 1))
                for h in range(HG):
                    dst, slots = bank_s[:, M * h:M * h + M], slice(M * h, M * h + M)
                    mm = pe.matmul(dst, masked[:, P * h:P * h + P], es[now][:, slots], start=True, stop=c == 0)
                    if c:
                        mm = pe.matmul(dst, qT[:, P * h:P * h + P], s1[:, slots], start=False, stop=True)
                mm.then_inc(ok_mm, 1)
                pe.wait_ge(gate_made, i)
                if last and c == CB - 1:
                    w_ready(g * 4 + 6)
                project(WK, bank_kg, nxt).then_inc(k_mm, 1)
                pe.wait_ge(q_summed, n)
                transposes(q_rot).then_inc(qT_mm, 1)
                pe.wait_ge(ok_scaled, i)
                pe.wait_ge(u_in[nxt], (u * 2 + ((c + 1) // 2 + 1)) * 16)
                pe.matmul(bank_s[:, 0:H], u_part[nxt][:, :], ws2_cols(g, last and c == CB - 1), start=True,
                          stop=True).then_inc(s_mm, 1)
                pe.wait_ge(o_norm_made, i)
                pe.wait_ge(qT_made, n)
                transposes(o_norm).then_inc(oT_mm, 1)
                pe.wait_ge(q_turned, n)
                if last and c == CB - 1:
                    w_ready(g * 4 + 7)
                project(WV, bank_qv, nxt).then_inc(v_mm, 1)
                pe.wait_ge(slot_p_made, i)
                pe.wait_ge(oT_lo_made, i)
                transposes(slot_p, HG // 2).then_inc(pT_mm, 1)
                if c == 1:
                    pe.wait_ge(wo_hi_made, u + 1)
                    pe.wait_ge(wo_lo_made, u + 1)
                for h in range(HG):
                    mm = product(bank_o[:, :], cols((oT_hi, oT_lo), P * h, P), cols((wo_hi, wo_lo), D * h, D),
                                 start=h == 0, stop=h == HG - 1)
                mm.then_inc(out_mm, 1)
                pe.wait_ge(pT_made, i)
                for r in range(HG // 2):
                    two = slice(2 * P * r, 2 * P * r + 2 * P)
                    mm = pe.matmul(bank_a[:, two], esT[:, P * r:P * r + P], pT[:, two], start=True, stop=True)
                mm.then_inc(w2_mm, 1)
                pe.wait_ge(es_made, n)
                transposes(es[nxt], HG // 2).then_inc(esT_mm, 1)
                pe.wait_ge(k_turned, n)
                if last and c == CB - 1:
                    w_ready(g * 4 + 8)
                project(WG, bank_kg, nxt).then_inc(g_mm, 1)
                pe.wait_ge(k_summed, n)
                pe.wait_ge(esT_made, n)
                transposes(k_rot[nxt]).then_inc(kT_mm, 1)
                running_sum(nxt, n, c == CB - 1)
                pe.wait_ge(w2_masked, i)
                pe.wait_ge(part_made, i)
                if c:
                    pe.wait_ge(s2_made, carried(u, c - 1))
                for h in range(HG):
                    dst, head = bank_o[:, DV * h:DV * h + DV], slice(P * h, P * h + P)
                    mm = pe.matmul(dst, masked[:, head], v[now][:, head], start=True, stop=c == 0)
                    if c:
                        mm = pe.matmul(dst, pT[:, head], s2[:, DV * (h // 2):DV * (h // 2) + DV], start=False,
                                       stop=True)
                mm.then_inc(o_mm, 1)
                if c < CB - 1:
                    pe.wait_ge(enz_made, n)
                    for h in range(HG):
                        mm = pe.matmul(s1_acc[:, M * h:M * h + M], k_rot[now][:, P * h:P * h + P],
                                       es[now][:, M * h:M * h + M], start=False, stop=True, skip_group_check=True)
                    mm.then_inc(s1_mm, 1)
                    for r in range(HG // 2):
                        two = slice(2 * DV * r, 2 * DV * r + 2 * DV)
                        mm = pe.matmul(bank_s2[:, two], es[now][:, P * r:P * r + P], v[now][:, two],
                                       start=c == 0 and r == 0, stop=True, skip_group_check=True)
                    mm.then_inc(s2_mm, 1)
                scores(n)

            def ws2_cols(g, next_group):
                g = (g + 1) % GROUPS if next_group else g
                return ws2_part[:, bass.ds(g * H, H)]

            all_steps(pe, step)
            pe.wait_ge(o_norm_made, STEPS + 1)
            transposes(o_norm).then_inc(oT_mm, 1)
            pe.wait_ge(oT_lo_made, STEPS + 1)
            for h in range(HG):
                mm = product(bank_o[:, :], cols((oT_hi, oT_lo), P * h, P), cols((wo_hi, wo_lo), D * h, D),
                             start=h == 0, stop=h == HG - 1)
            mm.then_inc(out_mm, 1)

            def front(j, s):
                pe.wait_ge(x1_made, j + 1)
                if not (isinstance(j, int) and j == 0):
                    pe.wait_ge(x1T_lo_made, j)
                transposes(x1[s]).then_inc(x1T_mm, 1)

            def back(j, s):
                pe.wait_ge(x1T_lo_made, j + 1)
                pe.wait_ge(wf_lo_made, 1)
                if not (isinstance(j, int) and j == 0):
                    pe.wait_ge(y_made, j)
                for k in range(KT):
                    mm = product(bank_o[:, :], cols((x1T_hi[s], x1T_lo[s]), P * k, P), cols((wf_hi, wf_lo), D * k, D),
                                 start=k == 0, stop=k == KT - 1)
                mm.then_inc(ffn_mm, 1)

            last_phase(pe, front, back)


def kernel(**inputs):
    import numpy as np
    import concourse.bacc as bacc
    from concourse.bass_utils import run_bass_kernel_spmd

    def arr(name):
        return np.ascontiguousarray(inputs[name])

    hs = arr("L0_attn_hidden_states").reshape(CHUNKS, P, D)
    hs_cols = hs.reshape(CHUNKS, P, KT, P).transpose(0, 3, 2, 1).reshape(CHUNKS, P, KT * P)

    def grouped(w):
        return w.reshape(GROUPS, F, KT, P).transpose(0, 3, 2, 1).reshape(GROUPS, P, KT * F)

    wo = arr("L0_attn_Wo").reshape(D, GROUPS, HG, DV).transpose(1, 3, 2, 0).reshape(GROUPS, P, HG * D)
    w_groups = np.stack([grouped(arr("L0_attn_" + n)) for n in ("Wq", "Wk", "Wv", "Wg")] + [wo], axis=1)
    ws1 = np.zeros((P, KT, 4, 32), np.float32)
    ws1[:, :, :, :RANK] = arr("L0_attn_Ws1").reshape(RANK, KT, P).transpose(2, 1, 0)[:, :, None, :]
    ws2 = np.zeros((4, 32, HEADS * M), np.float32)
    ws2[:, :RANK] = arr("L0_attn_Ws2").T
    ws2[0::2, RANK] = arr("L0_attn_bs2")
    pos = np.arange(T, dtype=np.float32)
    inv_freq = (np.float32(1.0) / np.float32(10000.0) ** (np.arange(0, DK, 2, dtype=np.float32) / np.float32(DK)))
    ang = (pos[:, None] * inv_freq[None, :].astype(np.float32)).astype(np.float32)
    cos, sin = np.cos(ang).astype(np.float32), np.sin(ang).astype(np.float32)
    rope_cos = cos.reshape(CB, P, 64).transpose(1, 0, 2).reshape(P, CB * 64)
    rope_sin = np.concatenate([-sin, sin], axis=1).reshape(CB, P, 128).transpose(1, 0, 2).reshape(P, CB * 128)
    at = np.arange(P)
    keep_mask = (at[:, None] <= at[None, :]).astype(np.float32)
    arrays = {
        "hs_cols": hs_cols,
        "hs_rows": hs,
        "w_groups": w_groups,
        "ws1": ws1.reshape(P, KT * P),
        "ws2": ws2.reshape(P, HEADS * M),
        "gnorm": arr("L0_attn_g_norm_weight").reshape(P, 1),
        "ffn_w": arr("L0_ffn_weight").reshape(D, KT, P).transpose(2, 1, 0).reshape(P, KT * D),
        "ffn_scale": arr("L0_ffn_scale_weight"),
        "ffn_bias": arr("L0_ffn_bias"),
        "rope_cos": rope_cos,
        "rope_sin": rope_sin,
        "keep_mask": keep_mask,
        "below_mask": 1 - keep_mask,
        "identity": np.eye(P, dtype=np.float32),
    }
    arrays = {n: np.ascontiguousarray(a) for n, a in arrays.items()}
    nc = bacc.Bacc("TRN2", target_bir_lowering=False, num_devices=1)
    args = [nc.dram_tensor(n, a.shape, mybir.dt.from_np(a.dtype), kind="ExternalInput").ap() for n, a in arrays.items()]
    out = nc.dram_tensor("out", (CHUNKS, P, D), F32, kind="ExternalOutput").ap()
    gated_slot_attention_block(nc, *args, out)
    result = run_bass_kernel_spmd(nc, [arrays], core_ids=[0])
    return result.results[0]["out"].reshape(BATCH, T, D)
```

```python
from contextlib import ExitStack

import concourse.bass as bass
from concourse import mybir

P = 128
BATCH, T, D = 4, 512, 512
HEADS, DK, DV, M = 16, 128, 128, 64
RANK = 16
HG = 4
GROUPS = HEADS // HG
CB = T // P
CHUNKS = BATCH * CB
STEPS = GROUPS * CHUNKS
KT = D // P
F = HG * DK
H = HG * M
CLAMP, EPS = 32.0, 1e-5
SCALE = DK ** -0.5
WQ, WK, WV, WG, WO = range(5)

F32 = mybir.dt.float32
F32R = mybir.dt.float32r
ALU = mybir.AluOpType
ACT = mybir.ActivationFunctionType
AX = mybir.AxisListType


SMALL = {}
for name, width in (("cos", CB * 64), ("sin", CB * 128), ("keep", P), ("below", P), ("identity", P), ("gnorm", 1),
                    ("ws2", HEADS * M)):
    start = sum(stop - first for first, stop in SMALL.values())
    SMALL[name] = (start, start + width)
SMALL_COLS = SMALL["ws2"][1]


def gated_slot_attention_block(nc, hs_cols, hs_rows, w_groups, ws1, small_in, ffn_w, ffn_scale, ffn_bias, out):
    with ExitStack() as ctx:
        def sb(name, cols, dt=F32):
            return ctx.enter_context(nc.sbuf_tensor(name, [P, cols], dt))

        def bank(name):
            return ctx.enter_context(nc.psum_tensor(name, [P, 512], F32))

        def sem(name):
            return ctx.enter_context(nc.semaphore(name))

        u_dram = nc.dram_tensor("u_scratch", (CHUNKS, P, P), F32, kind="Internal").ap()
        x_dram = nc.dram_tensor("x_scratch", (1 + CHUNKS + STEPS, P, D), F32, kind="Internal").ap()

        w_hi = [sb(f"w_hi{m}", KT * F, F32R) for m in range(4)]
        w_lo = [sb(f"w_lo{m}", KT * F, F32R) for m in range(4)]
        wo_hi, wo_lo = sb("wo_hi", HG * D, F32R), sb("wo_lo", HG * D, F32R)
        w_raw = [sb(f"w_raw{s}", KT * F) for s in range(2)]
        ws2_part = sb("ws2_part", HEADS * M, F32R)
        wf_hi, wf_lo = sb("wf_hi", KT * D, F32R), sb("wf_lo", KT * D, F32R)
        small = sb("small_ops", SMALL_COLS)
        cos_t, sin_t, keep, below_raw, ident, gn, ws2_raw = [small[:, a:b] for a, b in SMALL.values()]
        keep_r, below_r = sb("keep_r", P, F32R), sb("below_r", P, F32R)
        minus_half = sb("minus_half", HG)
        batch_raw = [sb(f"batch_raw{s}", KT * T) for s in range(2)]
        ws1_raw = sb("ws1_raw", KT * P)
        ws2_low = sb("ws2_low", HEADS * M, F32R)
        masked, o_sq, qT, kT = [batch_raw[0][:, F * k:F * k + F] for k in range(4)]
        v = [batch_raw[1][:, F * k:F * k + F] for k in (0, 1)]
        gate = [batch_raw[1][:, F * k:F * k + F] for k in (2, 3)]
        ok, slot_p = ws1_raw[:, 0:H], ws1_raw[:, H:2 * H]
        s1, s_clip, *es = [ws2_raw[:, H * k:H * k + H] for k in range(4)]
        v_hi = [ws2_low[:, F * k:F * k + F] for k in (0, 1)]
        hs_raw = [sb(f"hs_raw{s}", KT * P) for s in range(2)]
        hs_hi = [sb(f"hs_hi{s}", KT * P, F32R) for s in range(2)]
        hs_lo = [sb(f"hs_lo{s}", KT * P, F32R) for s in range(2)]
        u_part = [sb(f"u_part{s}", P, F32R) for s in range(2)]
        rope_a, rope_b, q_rot = sb("rope_a", F), sb("rope_b", F), sb("q_rot", F)
        k_rot = [sb(f"k_rot{s}", F) for s in range(2)]
        v_lo = [sb(f"v_lo{s}", F, F32R) for s in range(2)]
        es_hi = [sb(f"es_hi{s}", H, F32R) for s in range(2)]
        es_lo = [sb(f"es_lo{s}", H, F32R) for s in range(2)]
        esT_hi, esT_lo = sb("esT_hi", H, F32R), sb("esT_lo", H, F32R)
        enz = sb("enz", H)
        ok_max, p_sum, sum_sq = sb("ok_max", HG), sb("p_sum", HG), sb("sum_sq", HG)
        eps_sum, var, rms = sb("eps_sum", HG), sb("var", HG), sb("rms", HG)
        pT_hi, pT_lo = sb("pT_hi", F, F32R), sb("pT_lo", F, F32R)
        pair_pT_hi, pair_pT_lo = sb("pair_pT_hi", H, F32R), sb("pair_pT_lo", H, F32R)
        s2_hi, s2_lo = sb("s2_hi", HG * DV, F32R), sb("s2_lo", HG * DV, F32R)
        o_gated = sb("o_gated", F)
        oT_hi, oT_lo = sb("oT_hi", F, F32R), sb("oT_lo", F, F32R)
        part = [sb(f"part{s}", D) for s in range(2)]

        bank_qv, bank_kg, bank_t, bank_a, bank_s, bank_c, bank_s2, bank_o = [
            bank(n) for n in ("bank_qv", "bank_kg", "bank_t", "bank_a", "bank_s", "bank_c", "bank_s2", "bank_o")]
        cums, s1_acc = bank_c[:, 0:H], bank_c[:, H:2 * H]

        LAST = 4
        bias_row = rope_b

        def quarters(t):
            return [t[:, D * s:D * s + D] for s in range(LAST)]

        x_row, x1, x1T_hi, x1T_lo = [quarters(t) for t in (w_raw[1], w_raw[0], w_hi[2], w_lo[2])]
        x1_bias, y_row, z = [[t[:, :] for t in four] for four in (
            (q_rot, k_rot[0], k_rot[1], qT), (kT, v[0], v[1], o_sq), (gate[0], gate[1], masked, rope_a))]
        banks_T, banks_ffn = (bank_c, bank_s2, bank_s, bank_a), (bank_qv, bank_kg, bank_t, bank_o)
        FIRST, SECOND = 0, 1
        STATS, MEAN_VAR, VAR_EPS, NEG_MEAN, RSTD, SHIFT, ROWS = range(7)
        norms = []
        for name in ("first", "second"):
            norms.append([[sb(f"{name}_{what}{s}", n) for s in range(LAST)] for what, n in
                          (("stats", 6), ("mean_var", 2), ("var_eps", 1), ("neg_mean", 1), ("rstd", 1), ("shift", 1))])

        const_in, ws1_in, scale_in = sem("const_in"), sem("ws1_in"), sem("scale_in")
        batch_in, part_in = [sem(f"batch_in{s}") for s in range(2)], [sem(f"part_in{s}") for s in range(2)]
        stored = [sem(f"stored{s}") for s in range(2)]
        hs_in, u_in = [sem(f"hs_in{s}") for s in range(2)], [sem(f"u_in{s}") for s in range(2)]
        w_in = [sem(f"w_in{s}") for s in range(2)]
        zeroed, ones_set, consts_made, ws2_made = sem("zeroed"), sem("ones_set"), sem("consts_made"), sem("ws2_made")
        u_mm, u_hi_made, u_made = sem("u_mm"), sem("u_hi_made"), sem("u_made")
        hs_hi_made, hs_lo_made = sem("hs_hi_made"), sem("hs_lo_made")
        w_hi_made, w_lo_made, wo_hi_made, wo_lo_made = (
            sem("w_hi_made"), sem("w_lo_made"), sem("wo_hi_made"), sem("wo_lo_made"))
        q_mm, k_mm, v_mm, g_mm, s_mm, out_mm = [sem(n) for n in ("q_mm", "k_mm", "v_mm", "g_mm", "s_mm", "out_mm")]
        a_mm, ok_mm, w2_mm, o_mm, s1_mm, s2_mm, cums_mm = [
            sem(n) for n in ("a_mm", "ok_mm", "w2_mm", "o_mm", "s1_mm", "s2_mm", "cums_mm")]
        qT_mm, kT_mm, pT_mm, esT_mm, oT_mm = [sem(n) for n in ("qT_mm", "kT_mm", "pT_mm", "esT_mm", "oT_mm")]
        q_turned, q_summed, k_turned, k_summed = [sem(n) for n in ("q_turned", "q_summed", "k_turned", "k_summed")]
        qT_made, kT_made, v_made, v_hi_made, v_lo_made, s1_made, s2_hi_made, s2_lo_made, a_masked, w2_masked = [
            sem(n) for n in ("qT_made", "kT_made", "v_made", "v_hi_made", "v_lo_made", "s1_made", "s2_hi_made",
                             "s2_lo_made", "a_masked", "w2_masked")]
        th_made, gate_made, s_clipped, es_made, es_hi_made, es_lo_made, esT_hi_made, esT_lo_made, enz_made = [
            sem(n) for n in ("th_made", "gate_made", "s_clipped", "es_made", "es_hi_made", "es_lo_made",
                             "esT_hi_made", "esT_lo_made", "enz_made")]
        ok_scaled, ok_maxed, ok_shifted, prob_made, prob_summed, slot_p_made, pT_hi_made, pT_lo_made = [
            sem(n) for n in ("ok_scaled", "ok_maxed", "ok_shifted", "prob_made", "prob_summed", "slot_p_made",
                             "pT_hi_made", "pT_lo_made")]
        o_squared, sq_summed, eps_scaled, var_made, rms_made, o_gated_made, o_norm_made = [
            sem(n) for n in ("o_squared", "sq_summed", "eps_scaled", "var_made", "rms_made", "o_gated_made",
                             "o_norm_made")]
        oT_hi_made, oT_lo_made, part_made = sem("oT_hi_made"), sem("oT_lo_made"), sem("part_made")
        bias_in, wf_scaled_made, wf_hi_made, wf_lo_made = [
            sem(n) for n in ("bias_in", "wf_scaled_made", "wf_hi_made", "wf_lo_made")]
        x_in = [sem(f"x_in{s}") for s in range(LAST)]
        z_out = [sem(f"z_out{s}") for s in range(LAST)]
        norm_sems = [[sem(f"{name}_{what}_made") for what in
                      ("stats", "mean_var", "var_eps", "neg_mean", "rstd", "shift", "rows")]
                     for name in ("first", "second")]
        biased_made, x1T_mm, x1T_hi_made, x1T_lo_made, ffn_mm, y_made = [
            sem(n) for n in ("biased_made", "x1T_mm", "x1T_hi_made", "x1T_lo_made", "ffn_mm", "y_made")]
        x_copied = sem("x_copied")

        U_STORES = BATCH // 2
        LOOP_STORES = [U_STORES + STEPS // 2 + 1, U_STORES + STEPS // 2]

        def done(u, c, ahead=0):
            return u * CB + (c + 1 + ahead)

        def carried(u, c):
            return u * (CB - 1) + (c + 1)

        def all_steps(eng, body):
            def group(g, changes):
                with eng.Fori(0, BATCH - 1) as b:
                    for c in range(CB):
                        body(g * BATCH + b, g, b, c, False, CB)
                for c in range(CB):
                    body(g * BATCH + (BATCH - 1), g, BATCH - 1, c, changes, CB if changes else CB - 1 - c)

            with eng.Fori(0, GROUPS - 1) as g:
                group(g, True)
            group(GROUPS - 1, False)

        SLOT = {WQ: 1, WK: 0, WV: 1, WG: 0, WO: 0}

        def raw_in(m, g, b=0):
            if m == WO:
                return g * 6 + b + 3
            if SLOT[m] == 0:
                return g * 6 + (1 if m == WK else 2)
            return g * 2 + (1 if m == WQ else 2)

        def next_raw_in(m, g):
            return g * 6 + (7 if m == WK else 8) if SLOT[m] == 0 else g * 2 + (4 if m == WQ else 5)

        def per_head(ap, n=HG):
            return ap.rearrange("p (h x) -> p h x", h=n)

        def over_heads(ap, n=HG):
            return ap.unsqueeze(1).broadcast_to([P, n, ap.shape[1]])

        def over_columns(ap, n):
            return ap.unsqueeze(2).broadcast_to([P, ap.shape[1], n])

        def of_pair(ap, half, n):
            return ap[64 * half:64 * half + 64, :].rearrange("p (r e x) -> p r e x", e=2, x=n)[:, :, half, :]

        def last_phase(eng, lag_max, tick, before=LAST, after={}):
            for t in range(LAST, before):
                tick(t, t % LAST)
                if t in after:
                    after[t]()
            with eng.Fori(before // LAST, CHUNKS // LAST) as r:
                for s in range(LAST):
                    tick(r * LAST + s, s)
            for t in range(CHUNKS, CHUNKS + lag_max):
                tick(t, t % LAST)

        def staged(t, s, lag):
            return t - lag, (s - lag) % LAST, not isinstance(t, int) or 0 <= t - lag < CHUNKS

        block = ctx.enter_context(nc.Block())

        @block.sync
        def _(sp):
            def load_batch(b):
                sp.dma_start(batch_raw[b % 2][:, :].rearrange("p (c x) -> p c x", c=CB),
                             hs_cols[CB * b:CB * b + CB].rearrange("c p x -> p c x")).then_inc(batch_in[b % 2], 16)

            def store_u(b):
                sp.wait_ge(u_made, b + 1)
                sp.dma_start(u_dram[CB * b:CB * b + CB].rearrange("c p t -> p c t"),
                             part[b % 2][:, :].rearrange("p (c t) -> p c t", c=CB)).then_inc(stored[b % 2], 16)

            def load_hs(slot, chunk):
                sp.dma_start(hs_raw[slot][:, :], hs_cols[chunk]).then_inc(hs_in[slot], 16)

            def load_u(slot, chunk):
                sp.dma_start(u_part[slot][:, :].bitcast(F32), u_dram[chunk]).then_inc(u_in[slot], 16)

            def load_x(slot, row):
                sp.dma_start(part[slot][:, :], row).then_inc(part_in[slot], 16)

            def load_w(m, g):
                sp.dma_start(w_raw[SLOT[m]][:, :], w_groups[g, m]).then_inc(w_in[SLOT[m]], 16)

            def w_split(count):
                sp.wait_ge(w_hi_made, count)
                sp.wait_ge(w_lo_made, count)

            sp.dma_start(ws1_raw[:, :], ws1).then_inc(ws1_in, 16)
            load_batch(0)
            load_hs(0, 0)
            load_batch(1)
            load_w(WQ, 0)
            sp.dma_start(small[:, :], small_in).then_inc(const_in, 16)
            load_w(WK, 0)
            load_hs(1, 1)
            store_u(0)
            load_batch(2)
            w_split(1)
            load_w(WV, 0)
            store_u(1)
            load_batch(3)
            w_split(2)
            load_w(WG, 0)
            sp.wait_ge(stored[0], 16)
            for s in range(2):
                load_u(s, s)
            sp.dma_start(k_rot[1][:, :], ffn_scale.partition_broadcast(P)).then_inc(scale_in, 16)
            store_u(2)
            w_split(3)
            sp.dma_start(w_raw[1][:, :], ffn_w).then_inc(w_in[1], 16)
            store_u(3)
            for s in range(2):
                sp.wait_ge(stored[s], 16 * U_STORES)
            load_x(0, hs_rows[CHUNKS - 1])
            w_split(4)
            load_w(WO, 0)
            sp.dma_start(x_dram[1:CHUNKS], hs_rows[:CHUNKS - 1]).then_inc(x_copied, 16)
            sp.wait_ge(wf_hi_made, 1)
            sp.wait_ge(wf_lo_made, 1)

            def load_row(j, s):
                sp.dma_start(x_row[s], x_dram[j + (1 + STEPS)]).then_inc(x_in[s], 16)

            def row_free(j):
                sp.wait_ge(norm_sems[FIRST][ROWS], j + (1 - LAST))

            def step(u, g, b, c, last, left):
                if not left:
                    for j in range(LAST):
                        load_row(j, j)
                    sp.wait_ge(k_summed, STEPS)
                    sp.dma_start(bias_row[:, :], ffn_bias.partition_broadcast(P)).then_inc(bias_in, 16)
                chunk = c - 2 if last and c >= 2 else b * CB + (c + 2)
                if left >= 2:
                    sp.wait_ge(hs_hi_made, done(u, c))
                    sp.wait_ge(hs_lo_made, done(u, c))
                    load_hs(c % 2, chunk)
                    sp.wait_ge(s_mm, done(u, c))
                    load_u(c % 2, chunk)
                if c == 1 and left >= CB:
                    sp.wait_ge(wo_hi_made, u + 1)
                    sp.wait_ge(wo_lo_made, u + 1)
                    if last:
                        load_w(WQ, g + 1)
                        load_w(WK, g + 1)
                    else:
                        load_w(WO, g)
                if c == 2 and last:
                    w_split(g * 4 + 5)
                    load_w(WV, g + 1)
                    w_split(g * 4 + 6)
                    load_w(WG, g + 1)
                sp.wait_ge(stored[(c + 1) % 2], (u * (CB // 2) + ((c + 1) // 2 + U_STORES)) * 16)
                sp.wait_ge(x_copied, 16)
                load_x((c + 1) % 2, x_dram[u * CB + (c + 1)])
                sp.wait_ge(part_made, done(u, c))
                sp.dma_start(x_dram[u * CB + (c + CHUNKS)], part[c % 2][:, :]).then_inc(stored[c % 2], 16)
                if c == 3 and last:
                    w_split(g * 4 + 8)
                    load_w(WO, g + 1)

            all_steps(sp, step)

            for j in range(LAST, 2 * LAST):
                row_free(j)
                load_row(j, j % LAST)
            sp.wait_ge(part_made, STEPS + 1)
            sp.dma_start(x_dram[STEPS + CHUNKS], part[0][:, :]).then_inc(stored[0], 16)
            for s in range(2):
                sp.wait_ge(stored[s], 16 * LOOP_STORES[s])
            with sp.Fori(2, CHUNKS // LAST) as r:
                for s in range(LAST):
                    row_free(r * LAST + s)
                    load_row(r * LAST + s, s)
            for s in range(LAST):
                sp.wait_ge(z_out[s], 16 * CHUNKS // LAST)

        @block.gpsimd
        def _(pool):
            for t in part:
                pool.memset(t[:, :], 1.0).then_inc(ones_set, 1)
            for t in (wo_hi, wo_lo, pT_hi, pT_lo, s2_hi, s2_lo):
                pool.memset(t[:, :].bitcast(F32), 0.0).then_inc(zeroed, 1)
            pool.memset(o_gated[:, :], 0.0).then_inc(o_gated_made, 1)
            pool.memset(var[:, :], 1.0).then_inc(var_made, 1)
            pool.memset(minus_half[:, :], -0.5).then_inc(zeroed, 1)

            def v_split(slot, n):
                pool.wait_ge(v_hi_made, n)
                pool.tensor_tensor(v_lo[slot][:, :], v[slot][:, :], v_hi[slot][:, :].bitcast(F32),
                                   ALU.subtract).then_inc(v_lo_made, 1)

            def hs_split(slot, n):
                pool.wait_ge(hs_hi_made, n)
                pool.tensor_tensor(hs_lo[slot][:, :], hs_raw[slot][:, :], hs_hi[slot][:, :].bitcast(F32),
                                   ALU.subtract).then_inc(hs_lo_made, 1)

            def q_sum(n):
                pool.wait_ge(q_turned, n)
                pool.tensor_tensor(q_rot[:, :], rope_a[:, :], rope_b[:, :], ALU.add).then_inc(q_summed, 1)

            def k_sum(slot, n):
                pool.wait_ge(k_turned, n)
                pool.tensor_tensor(k_rot[slot][:, :], rope_a[:, :], rope_b[:, :], ALU.add).then_inc(k_summed, 1)

            def es_split(slot, n):
                pool.wait_ge(es_hi_made, n)
                pool.tensor_tensor(es_lo[slot][:, :], es[slot][:, :], es_hi[slot][:, :].bitcast(F32),
                                   ALU.subtract).then_inc(es_lo_made, 1)

            hs_split(0, 1)
            q_sum(1)
            hs_split(1, 2)
            k_sum(0, 1)
            es_split(0, 1)
            v_split(0, 1)
            pool.wait_ge(zeroed, 7)

            def tick(t, s):
                j, slot, there = staged(t, s, 2)
                if there:
                    pool.wait_ge(norm_sems[FIRST][ROWS], j + 1)
                    pool.tensor_tensor(x1_bias[slot], x1[slot], bias_row[:, :], ALU.add).then_inc(biased_made, 1)
                for which, lag in ((FIRST, 0), (SECOND, 4)):
                    j, slot, there = staged(t, s, lag)
                    if there:
                        var_eps, rstd = norms[which][VAR_EPS][slot], norms[which][RSTD][slot]
                        pool.wait_ge(norm_sems[which][VAR_EPS], j + 1)
                        pool.tensor_tensor(rstd[:, :], var_eps[:, :], minus_half[:, 0:1], ALU.pow
                                           ).then_inc(norm_sems[which][RSTD], 1)

            def step(u, g, b, c, last, left):
                pool.wait_ge(o_gated_made, done(u, c))
                pool.wait_ge(var_made, done(u, c))
                pool.tensor_tensor(rms[:, :], var[:, :], minus_half[:, :], ALU.pow).then_inc(rms_made, 1)
                pool.wait_ge(rms_made, done(u, c))
                pool.tensor_tensor(per_head(o_gated[:, :]), per_head(o_gated[:, :]), over_columns(rms[:, :], DV),
                                   ALU.mult).then_inc(o_norm_made, 1)
                if left:
                    q_sum(done(u, c, 1))
                else:
                    tick(0, 0)
                pool.wait_ge(ok_maxed, done(u, c))
                pool.tensor_tensor(per_head(ok[:, :]), per_head(ok[:, :]), over_columns(ok_max[:, :], M),
                                   ALU.subtract).then_inc(ok_shifted, 1)
                pool.wait_ge(prob_made, done(u, c))
                pool.tensor_tensor(slot_p[:, :], ok[:, :], enz[:, :], ALU.mult).then_inc(slot_p_made, 1)
                if left:
                    k_sum((c + 1) % 2, done(u, c, 1))
                    es_split((c + 1) % 2, done(u, c, 1))
                    v_split((c + 1) % 2, done(u, c, 1))
                else:
                    tick(1, 1)
                    pool.wait_ge(bias_in, 16)
                    tick(2, 2)
                    tick(3, 3)
                if left >= 2:
                    hs_split(c % 2, done(u, c, 2))

            all_steps(pool, step)
            pool.wait_ge(o_gated_made, STEPS + 1)
            pool.wait_ge(var_made, STEPS + 1)
            pool.tensor_tensor(rms[:, :], var[:, :], minus_half[:, :], ALU.pow).then_inc(rms_made, 1)
            pool.wait_ge(rms_made, STEPS + 1)
            pool.tensor_tensor(per_head(o_gated[:, :]), per_head(o_gated[:, :]), over_columns(rms[:, :], DV),
                               ALU.mult).then_inc(o_norm_made, 1)

            last_phase(pool, 4, tick)

        @block.scalar
        def _(act):
            def copy(dst, src, scale=1.0):
                return act.activation(dst, src, ACT.Copy, scale=scale)

            def split_u(b):
                u_bank = bank_a if b % 2 else bank_s
                act.wait_ge(u_mm, b + 1)
                if b >= 2:
                    act.wait_ge(stored[b % 2], 16 * (b // 2))
                if b:
                    act.wait_ge(u_made, b)
                copy(oT_hi[:, :], u_bank[:, :])
                copy(part[b % 2][0:RANK, :].bitcast(F32R), u_bank[0:RANK, :])
                copy(part[b % 2][64:64 + RANK, :].bitcast(F32R), u_bank[64:64 + RANK, :]).then_inc(u_hi_made, 1)

            def w_split(m, loads):
                act.wait_ge(w_in[SLOT[m]], 16 * loads)
                copy(w_hi[m][:, :], w_raw[SLOT[m]][:, :]).then_inc(w_hi_made, 1)

            def hs_split(slot, n_in):
                act.wait_ge(hs_in[slot], n_in)
                copy(hs_hi[slot][:, :], hs_raw[slot][:, :]).then_inc(hs_hi_made, 1)

            def exp_s(slot, n):
                act.wait_ge(s_clipped, n)
                act.activation(es[slot][:, :], s_clip[:, :], ACT.Exp).then_inc(es_made, 1)
                act.wait_ge(es_made, n)
                copy(es_hi[slot][:, :], es[slot][:, :]).then_inc(es_hi_made, 1)

            def from_bank(dst, src, wait, n, made):
                act.wait_ge(wait, n)
                copy(dst, src).then_inc(made, 1)

            def v_split(slot, n):
                act.wait_ge(v_made, n)
                copy(v_hi[slot][:, :], v[slot][:, :]).then_inc(v_hi_made, 1)

            act.wait_ge(ones_set, 2)
            hs_split(0, 16)
            split_u(0)
            w_split(WQ, raw_in(WQ, 0))
            split_u(1)
            act.wait_ge(const_in, 16)
            copy(keep_r[:, :], keep).then_inc(consts_made, 1)
            copy(below_r[:, :], below_raw).then_inc(consts_made, 1)
            copy(ws2_part[0:64, :], ws2_raw[0:64, :]).then_inc(ws2_made, 1)
            copy(ws2_low[64:128, :], ws2_raw[64:128, :]).then_inc(ws2_made, 1)
            w_split(WK, raw_in(WK, 0))
            w_split(WV, raw_in(WV, 0))
            split_u(2)
            w_split(WG, raw_in(WG, 0))
            split_u(3)
            hs_split(1, 16)
            act.wait_ge(zeroed, 7)
            from_bank(qT[:, :], bank_t[:, :], qT_mm, 1, qT_made)
            exp_s(0, 1)
            from_bank(v[0][:, :], bank_qv[:, :], v_mm, 1, v_made)
            v_split(0, 1)
            act.wait_ge(g_mm, 1)
            act.activation(gate[0][:, :], bank_kg[:, :], ACT.Tanh, scale=0.5).then_inc(th_made, 1)
            from_bank(esT_hi[:, :], bank_t[:, 0:H], esT_mm, 1, esT_hi_made)
            from_bank(kT[:, :], bank_t[:, :], kT_mm, 1, kT_made)
            act.wait_ge(wf_scaled_made, KT)
            copy(wf_hi[:, :], w_raw[1][:, :]).then_inc(wf_hi_made, 1)

            def rows(which, j, slot, src, dst):
                neg_mean, rstd, shift = [norms[which][k][slot] for k in (NEG_MEAN, RSTD, SHIFT)]
                act.wait_ge(norm_sems[which][RSTD], j + 1)
                act.activation(shift[:, :], neg_mean[:, :], ACT.Copy, scale=rstd[:, 0:1]
                               ).then_inc(norm_sems[which][SHIFT], 1)
                act.wait_ge(norm_sems[which][SHIFT], j + 1)
                act.activation(dst, src, ACT.Identity, bias=shift[:, 0:1], scale=rstd[:, 0:1]
                               ).then_inc(norm_sems[which][ROWS], 1)

            def tick(t, s):
                j, slot, there = staged(t, s, 1)
                if there:
                    act.wait_ge(x1T_mm, j + 1)
                    copy(x1T_hi[slot], banks_T[slot][:, :]).then_inc(x1T_hi_made, 1)
                j, slot, there = staged(t, s, 0)
                if there:
                    rows(FIRST, j, slot, x_row[slot], x1[slot])
                j, slot, there = staged(t, s, 4)
                if there:
                    if not isinstance(j, int) or j >= LAST:
                        act.wait_ge(z_out[slot], (j - slot) * (16 // LAST))
                    rows(SECOND, j, slot, y_row[slot], z[slot])
                    act.wait_ge(norm_sems[SECOND][ROWS], j + 1)
                    act.dma_start(out[j], z[slot]).then_inc(z_out[slot], 16)

            def step(u, g, b, c, last, left):
                i, n = done(u, c), done(u, c, 1)
                if not left:
                    tick(0, 0)
                from_bank(oT_hi[:, :], bank_t[:, :], oT_mm, i, oT_hi_made)
                act.wait_ge(ok_shifted, i)
                act.activation(ok[:, :], ok[:, :], ACT.Exp).then_inc(prob_made, 1)
                if last and c == 2:
                    act.wait_ge(q_mm, n)
                    w_split(WQ, next_raw_in(WQ, g))
                if last and c == 3:
                    w_split(WG, next_raw_in(WG, g))
                if left:
                    from_bank(qT[:, :], bank_t[:, :], qT_mm, n, qT_made)
                    exp_s((c + 1) % 2, n)
                    from_bank(v[(c + 1) % 2][:, :], bank_qv[:, :], v_mm, n, v_made)
                act.wait_ge(pT_mm, i)
                copy(of_pair(pT_hi[:, :], 0, P), per_head(bank_t[0:64, 0:H], 2))
                copy(of_pair(pT_hi[:, :], 1, P), per_head(bank_t[64:128, 0:H], 2))
                copy(pair_pT_hi[:, :], bank_t[:, 0:H]).then_inc(pT_hi_made, 1)
                if left:
                    v_split((c + 1) % 2, n)
                if last and c == 2:
                    w_split(WK, next_raw_in(WK, g))
                if c == 0:
                    act.wait_ge(out_mm, i)
                    act.wait_ge(w_in[0], raw_in(WO, g, b) * 16)
                    copy(wo_hi[:, :], w_raw[0][:, :], gn).then_inc(wo_hi_made, 1)
                if left:
                    from_bank(esT_hi[:, :], bank_t[:, 0:H], esT_mm, n, esT_hi_made)
                    if last and c == 2:
                        w_split(WV, next_raw_in(WV, g))
                    act.wait_ge(g_mm, n)
                    act.activation(gate[(c + 1) % 2][:, :], bank_kg[:, :], ACT.Tanh, scale=0.5).then_inc(th_made, 1)
                    from_bank(kT[:, :], bank_t[:, :], kT_mm, n, kT_made)
                if not left:
                    tick(1, 1)
                    tick(2, 2)
                if left >= 2:
                    hs_split(c % 2, (u * (CB // 2) + (c // 2 + 2)) * 16)
                act.wait_ge(o_mm, i)
                act.activation(o_sq[:, :], bank_o[:, :], ACT.Square).then_inc(o_squared, 1)
                if c < CB - 1:
                    from_bank(s1[:, :], s1_acc, s1_mm, carried(u, c), s1_made)
                    act.wait_ge(s2_mm, carried(u, c))
                    copy(of_pair(s2_hi[:, :], 0, DV), of_pair(bank_s2[:, :], 0, DV))
                    copy(of_pair(s2_hi[:, :], 1, DV), of_pair(bank_s2[:, :], 1, DV)).then_inc(s2_hi_made, 1)

            all_steps(act, step)
            tick(3, 3)
            from_bank(oT_hi[:, :], bank_t[:, :], oT_mm, STEPS + 1, oT_hi_made)

            last_phase(act, 4, tick, before=2 * LAST)

        @block.vector
        def _(dve):
            def minus_hi(dst, src, hi):
                return dve.tensor_tensor(dst, src, hi.bitcast(F32), ALU.subtract)

            def split_u(b):
                dve.wait_ge(u_hi_made, b + 1)
                u_bank = bank_a if b % 2 else bank_s
                for q in (32, 96):
                    last = minus_hi(part[b % 2][q:q + RANK, :].bitcast(F32R), u_bank[q:q + RANK, :],
                                    oT_hi[q:q + RANK, :])
                last.then_inc(u_made, 1)

            def rotate(chunk, bank_in, turned, n):
                halves = "p (r x) -> p r x"
                x = bank_in[:, :].rearrange(halves, x=DK // 2)
                dve.tensor_tensor(rope_a[:, :].rearrange(halves, x=DK // 2), x,
                                  over_heads(cos_t[:, 64 * chunk:64 * chunk + 64], 2 * HG), ALU.mult)
                sins = sin_t[:, 128 * chunk:128 * chunk + 128]
                for half in range(2):
                    x = bank_in[:, :].rearrange("p (h e x) -> p h e x", e=2, x=DK // 2)[:, :, 1 - half, :]
                    y = rope_b[:, :].rearrange("p (h e x) -> p h e x", e=2, x=DK // 2)[:, :, half, :]
                    last = dve.tensor_tensor(y, x, over_heads(sins[:, 64 * half:64 * half + 64]), ALU.mult)
                last.then_inc(turned, 1)

            def rotate_q(chunk, n, first=False):
                dve.wait_ge(q_mm, n)
                if not first:
                    dve.wait_ge(k_summed, n - 1)
                rotate(chunk, bank_qv, q_turned, n)

            def rotate_k(chunk, n):
                dve.wait_ge(k_mm, n)
                dve.wait_ge(q_summed, n)
                rotate(chunk, bank_kg, k_turned, n)

            def w_split(m, n):
                dve.wait_ge(w_hi_made, n)
                minus_hi(w_lo[m][:, :], w_raw[SLOT[m]][:, :], w_hi[m][:, :]).then_inc(w_lo_made, 1)

            def lo(dst, src, hi, hi_made, n, made):
                dve.wait_ge(hi_made, n)
                minus_hi(dst, src, hi).then_inc(made, 1)

            def minus_pair(dst, hi, n, src):
                for half in range(2):
                    last = minus_hi(of_pair(dst[:, :], half, n), src(half), of_pair(hi[:, :], half, n))
                return last

            def esT_split(n):
                lo(esT_lo[:, :], bank_t[:, 0:H], esT_hi[:, :], esT_hi_made, n, esT_lo_made)

            def clip(n):
                dve.wait_ge(s_mm, n)
                dve.tensor_scalar(s_clip[:, :], bank_s[:, 0:H], CLAMP, -CLAMP, ALU.min, ALU.max).then_inc(s_clipped, 1)

            def make_gate(slot, n):
                dve.wait_ge(th_made, n)
                dve.scalar_tensor_tensor(gate[slot][:, :], gate[slot][:, :], 1.0, bank_kg[:, :], ALU.add, ALU.mult
                                         ).then_inc(gate_made, 1)

            def make_enz(n):
                dve.wait_ge(cums_mm, n)
                dve.reciprocal(enz[:, :], cums).then_inc(enz_made, 1)

            def mask(mm, n, made):
                dve.wait_ge(mm, n)
                dve.tensor_tensor(per_head(masked[:, :]), per_head(bank_a[:, :]), over_heads(keep), ALU.mult
                                  ).then_inc(made, 1)

            split_u(0)
            w_split(WQ, 1)
            split_u(1)
            dve.wait_ge(ws2_made, 2)
            minus_hi(ws2_part[64:128, :], ws2_raw[64:128, :], ws2_low[64:128, :]).then_inc(ws2_made, 1)
            w_split(WK, 2)
            dve.wait_ge(const_in, 16)
            rotate_q(0, 1, first=True)
            w_split(WV, 3)
            split_u(2)
            w_split(WG, 4)
            split_u(3)
            rotate_k(0, 1)
            clip(1)
            dve.wait_ge(w_in[1], 16 * 3)
            dve.wait_ge(scale_in, 16)
            for k in range(KT):
                cols = slice(D * k, D * k + D)
                dve.tensor_tensor(w_raw[1][:, cols], w_raw[1][:, cols], k_rot[1][:, :], ALU.mult
                                  ).then_inc(wf_scaled_made, 1)
            esT_split(1)
            make_enz(1)
            make_gate(0, 1)
            mask(a_mm, 1, a_masked)
            dve.wait_ge(wf_hi_made, 1)
            minus_hi(wf_lo[:, :], w_raw[1][:, :], wf_hi[:, :]).then_inc(wf_lo_made, 1)
            dve.wait_ge(zeroed, 7)

            def stats(which, slot, row):
                dve.bn_stats(norms[which][STATS][slot][:, :], row).then_inc(norm_sems[which][STATS], 1)

            def mean_var(which, slot):
                dve.bn_aggr(norms[which][MEAN_VAR][slot][:, :], norms[which][STATS][slot][:, :]
                            ).then_inc(norm_sems[which][MEAN_VAR], 1)

            def norm_factors(which, j, slot):
                moments, var_eps, neg_mean = [norms[which][k][slot] for k in (MEAN_VAR, VAR_EPS, NEG_MEAN)]
                dve.wait_ge(norm_sems[which][MEAN_VAR], j + 1)
                dve.tensor_scalar(neg_mean[:, :], moments[:, 0:1], -1.0, None, ALU.mult)
                dve.tensor_scalar(var_eps[:, :], moments[:, 1:2], EPS, None, ALU.add
                                  ).then_inc(norm_sems[which][VAR_EPS], 1)

            def tick(t, s):
                first, second, middle = [staged(t, s, lag) for lag in (0, 4, 2)]
                if first[2]:
                    j, slot, _ = first
                    dve.wait_ge(x_in[slot], (j - slot) * (16 // LAST) + 16)
                    stats(FIRST, slot, x_row[slot])
                if second[2]:
                    j, slot, _ = second
                    dve.wait_ge(ffn_mm, j + 1)
                    dve.wait_ge(biased_made, j + 1)
                    dve.tensor_tensor(y_row[slot], banks_ffn[slot][:, :], x1_bias[slot], ALU.add).then_inc(y_made, 1)
                    dve.wait_ge(y_made, j + 1)
                    stats(SECOND, slot, y_row[slot])
                if first[2]:
                    dve.wait_ge(norm_sems[FIRST][STATS], first[0] + 1)
                if second[2]:
                    dve.wait_ge(norm_sems[SECOND][STATS], second[0] + 1)
                if middle[2]:
                    j, slot, _ = middle
                    lo(x1T_lo[slot], banks_T[slot][:, :], x1T_hi[slot], x1T_hi_made, j + 1, x1T_lo_made)
                for which, (j, slot, there) in ((FIRST, first), (SECOND, second)):
                    if there:
                        mean_var(which, slot)
                for which, (j, slot, there) in ((FIRST, first), (SECOND, second)):
                    if there:
                        norm_factors(which, j, slot)

            def step(u, g, b, c, last, left):
                i, n = done(u, c), done(u, c, 1)
                if left:
                    rotate_q((c + 1) % CB, n)
                else:
                    tick(0, 0)
                dve.wait_ge(ok_mm, i)
                dve.scalar_tensor_tensor(ok[:, :], bank_s[:, 0:H], SCALE, enz[:, :], ALU.mult, ALU.mult
                                         ).then_inc(ok_scaled, 1)
                dve.wait_ge(ok_scaled, i)
                dve.tensor_reduce(ok_max[:, :], per_head(ok[:, :]), AX.X, ALU.max).then_inc(ok_maxed, 1)
                lo(oT_lo[:, :], bank_t[:, :], oT_hi[:, :], oT_hi_made, i, oT_lo_made)
                dve.wait_ge(prob_made, i)
                dve.tensor_reduce(p_sum[:, :], per_head(ok[:, :]), AX.X, ALU.add).then_inc(prob_summed, 1)
                if left:
                    rotate_k((c + 1) % CB, n)
                    clip(n)
                dve.wait_ge(prob_summed, i)
                dve.scalar_tensor_tensor(eps_sum[:, :], p_sum[:, :], 4 * EPS, p_sum[:, :], ALU.mult, ALU.mult
                                         ).then_inc(eps_scaled, 1)
                if last and c == 2:
                    w_split(WQ, g * 4 + 5)
                if last and c == 3:
                    w_split(WG, g * 4 + 8)
                dve.wait_ge(pT_hi_made, i)
                minus_pair(pT_lo, pT_hi, P, lambda half: per_head(bank_t[64 * half:64 * half + 64, 0:H], 2))
                minus_hi(pair_pT_lo[:, :], bank_t[:, 0:H], pair_pT_hi[:, :]).then_inc(pT_lo_made, 1)
                if not left:
                    tick(1, 1)
                dve.wait_ge(out_mm, i)
                dve.wait_ge(part_in[c % 2], (u * (CB // 2) + (c // 2 + 1)) * 16)
                dve.tensor_tensor(part[c % 2][:, :], bank_o[:, :], part[c % 2][:, :], ALU.add).then_inc(part_made, 1)
                if not left:
                    tick(2, 2)
                mask(w2_mm, i, w2_masked)
                if not left:
                    tick(3, 3)
                if left:
                    esT_split(n)
                if last and c == 2:
                    w_split(WK, g * 4 + 6)
                if left:
                    make_enz(n)
                    make_gate((c + 1) % 2, n)
                dve.wait_ge(o_squared, i)
                dve.wait_ge(oT_mm, i)
                dve.tensor_tensor(o_gated[:, :], bank_o[:, :], gate[c % 2][:, :], ALU.mult).then_inc(o_gated_made, 1)
                dve.tensor_reduce(sum_sq[:, :], per_head(o_sq[:, :]), AX.X, ALU.add).then_inc(sq_summed, 1)
                dve.wait_ge(sq_summed, i)
                dve.wait_ge(eps_scaled, i)
                dve.scalar_tensor_tensor(var[:, :], sum_sq[:, :], 4.0 / DV, eps_sum[:, :], ALU.mult, ALU.add
                                         ).then_inc(var_made, 1)
                if left:
                    mask(a_mm, n, a_masked)
                if c < CB - 1:
                    dve.wait_ge(s2_hi_made, carried(u, c))
                    minus_pair(s2_lo, s2_hi, DV, lambda half: of_pair(bank_s2[:, :], half, DV)
                               ).then_inc(s2_lo_made, 1)
                if c == 0:
                    dve.wait_ge(wo_hi_made, u + 1)
                    dve.scalar_tensor_tensor(wo_lo[:, :], w_raw[0][:, :], gn, wo_hi[:, :].bitcast(F32),
                                             ALU.mult, ALU.subtract).then_inc(wo_lo_made, 1)
                if last and c == 2:
                    w_split(WV, g * 4 + 7)

            all_steps(dve, step)

            def last_oT():
                lo(oT_lo[:, :], bank_t[:, :], oT_hi[:, :], oT_hi_made, STEPS + 1, oT_lo_made)

            def last_part():
                dve.wait_ge(out_mm, STEPS + 1)
                dve.wait_ge(part_in[0], (STEPS // 2 + 1) * 16)
                dve.tensor_tensor(part[0][:, :], bank_o[:, :], part[0][:, :], ALU.add).then_inc(part_made, 1)

            last_oT()
            last_phase(dve, 4, tick, before=2 * LAST, after={LAST: last_part})

        @block.tensor
        def _(pe):
            def product(dst, lhs, rhs, start=True, stop=True, **kw):
                for n, (x, y) in enumerate(((lhs[0], rhs[0]), (lhs[0], rhs[1]), (lhs[1], rhs[0]))):
                    mm = pe.matmul(dst, x, y, start=start and n == 0, stop=stop and n == 2, **kw)
                return mm

            def cols(pair, a, n):
                return tuple(t[:, a:a + n] for t in pair)

            def project(m, dst, slot):
                for k in range(KT):
                    mm = product(dst[:, :], cols((hs_hi[slot], hs_lo[slot]), P * k, P),
                                 cols((w_hi[m], w_lo[m]), F * k, F), start=k == 0, stop=k == KT - 1)
                return mm

            def transposes(src, n=HG):
                for h in range(n):
                    mm = pe.transpose(bank_t[:, P * h:P * h + P], src[:, P * h:P * h + P], ident)
                return mm

            def w_ready(n):
                pe.wait_ge(w_hi_made, n)
                pe.wait_ge(w_lo_made, n)

            def running_sum(slot, n, first):
                pe.wait_ge(es_hi_made, n)
                pe.wait_ge(es_lo_made, n)
                if not first:
                    for t in (es_hi, es_lo):
                        pe.matmul(cums, below_r[:, :], t[1 - slot][:, :], start=False, stop=False,
                                  skip_group_check=True)
                pe.matmul(cums, keep_r[:, :], es_hi[slot][:, :], start=first, stop=False, skip_group_check=True)
                pe.matmul(cums, keep_r[:, :], es_lo[slot][:, :], start=False, stop=True, skip_group_check=True
                          ).then_inc(cums_mm, 1)

            def scores(n):
                pe.wait_ge(kT_made, n)
                for h in range(HG):
                    mm = pe.matmul(bank_a[:, P * h:P * h + P], kT[:, P * h:P * h + P], qT[:, P * h:P * h + P],
                                   start=True, stop=True)
                mm.then_inc(a_mm, 1)

            def low_rank(b):
                pe.wait_ge(batch_in[b % 2], 16 * (b // 2 + 1))
                if b >= 2:
                    pe.wait_ge(u_made, b - 1)
                for k in range(KT):
                    mm = pe.matmul(per_head((bank_a if b % 2 else bank_s)[:, :], CB), ws1_raw[:, P * k:P * k + P],
                                   batch_raw[b % 2][:, :].rearrange("p (c k t) -> p c k t", c=CB, k=KT)[:, :, k, :],
                                   start=k == 0, stop=k == KT - 1)
                mm.then_inc(u_mm, 1)

            pe.wait_ge(ws1_in, 16)
            low_rank(0)
            low_rank(1)
            pe.wait_ge(hs_hi_made, 1)
            pe.wait_ge(hs_lo_made, 1)
            w_ready(1)
            project(WQ, bank_qv, 0).then_inc(q_mm, 1)
            low_rank(2)
            w_ready(2)
            project(WK, bank_kg, 0).then_inc(k_mm, 1)
            low_rank(3)
            pe.wait_ge(const_in, 16)
            pe.wait_ge(consts_made, 2)
            pe.wait_ge(q_summed, 1)
            transposes(q_rot).then_inc(qT_mm, 1)
            w_ready(3)
            project(WV, bank_qv, 0).then_inc(v_mm, 1)
            pe.wait_ge(u_in[0], 16)
            pe.wait_ge(ws2_made, 3)
            pe.wait_ge(u_made, BATCH)
            pe.matmul(bank_s[:, 0:H], u_part[0][:, :], ws2_part[:, 0:H], start=True, stop=True).then_inc(s_mm, 1)
            w_ready(4)
            pe.wait_ge(k_turned, 1)
            project(WG, bank_kg, 0).then_inc(g_mm, 1)
            pe.wait_ge(qT_made, 1)
            pe.wait_ge(es_made, 1)
            transposes(es[0], HG // 2).then_inc(esT_mm, 1)
            running_sum(0, 1, True)
            pe.wait_ge(k_summed, 1)
            pe.wait_ge(esT_lo_made, 1)
            transposes(k_rot[0]).then_inc(kT_mm, 1)
            scores(1)

            def tick(t, s):
                j, slot, there = staged(t, s, 2)
                if there:
                    pe.wait_ge(x1T_lo_made, j + 1)
                    for k in range(KT):
                        mm = product(banks_ffn[slot][:, :], cols((x1T_hi[slot], x1T_lo[slot]), P * k, P),
                                     cols((wf_hi, wf_lo), D * k, D), start=k == 0, stop=k == KT - 1)
                    mm.then_inc(ffn_mm, 1)
                j, slot, there = staged(t, s, 0)
                if there:
                    pe.wait_ge(norm_sems[FIRST][ROWS], j + 1)
                    for k in range(KT):
                        mm = pe.transpose(banks_T[slot][:, P * k:P * k + P], x1[slot][:, P * k:P * k + P], ident)
                    mm.then_inc(x1T_mm, 1)

            def step(u, g, b, c, last, left):
                i, n = done(u, c), done(u, c, 1)
                now, nxt = c % 2, (c + 1) % 2
                w_set = (g * 4 + 8) if last and c == CB - 1 else g * 4 + 4
                if left:
                    pe.wait_ge(hs_hi_made, n)
                    pe.wait_ge(hs_lo_made, n)
                    pe.wait_ge(v_made, i)
                    if last and c == CB - 1:
                        w_ready(g * 4 + 5)
                    project(WQ, bank_qv, nxt).then_inc(q_mm, 1)
                pe.wait_ge(a_masked, i)
                if c:
                    pe.wait_ge(s1_made, carried(u, c - 1))
                for h in range(HG):
                    dst, slots = bank_s[:, M * h:M * h + M], slice(M * h, M * h + M)
                    mm = pe.matmul(dst, masked[:, P * h:P * h + P], es[now][:, slots], start=True, stop=c == 0)
                    if c:
                        mm = pe.matmul(dst, qT[:, P * h:P * h + P], s1[:, slots], start=False, stop=True)
                mm.then_inc(ok_mm, 1)
                pe.wait_ge(o_norm_made, i)
                transposes(o_gated).then_inc(oT_mm, 1)
                if not left:
                    pe.wait_ge(wf_lo_made, 1)
                    tick(0, 0)
                if left:
                    pe.wait_ge(gate_made, i)
                    if last and c == CB - 1:
                        w_ready(g * 4 + 6)
                    project(WK, bank_kg, nxt).then_inc(k_mm, 1)
                    pe.wait_ge(q_summed, n)
                    pe.wait_ge(oT_lo_made, i)
                    transposes(q_rot).then_inc(qT_mm, 1)
                    pe.wait_ge(ok_scaled, i)
                    pe.wait_ge(u_in[nxt], (u * 2 + ((c + 1) // 2 + 1)) * 16)
                    pe.matmul(bank_s[:, 0:H], u_part[nxt][:, :], ws2_cols(g, last and c == CB - 1), start=True,
                              stop=True).then_inc(s_mm, 1)
                    pe.wait_ge(q_turned, n)
                    if last and c == CB - 1:
                        w_ready(g * 4 + 7)
                    project(WV, bank_qv, nxt).then_inc(v_mm, 1)
                pe.wait_ge(slot_p_made, i)
                if left:
                    pe.wait_ge(qT_made, n)
                else:
                    pe.wait_ge(oT_lo_made, i)
                transposes(slot_p, HG // 2).then_inc(pT_mm, 1)
                if c == 1:
                    pe.wait_ge(wo_hi_made, u + 1)
                    pe.wait_ge(wo_lo_made, u + 1)
                for h in range(HG):
                    mm = product(bank_o[:, :], cols((oT_hi, oT_lo), P * h, P), cols((wo_hi, wo_lo), D * h, D),
                                 start=h == 0, stop=h == HG - 1)
                mm.then_inc(out_mm, 1)
                pe.wait_ge(pT_lo_made, i)
                for r in range(HG // 2):
                    mm = product(bank_a[:, 2 * P * r:2 * P * r + 2 * P], cols((esT_hi, esT_lo), P * r, P),
                                 cols((pT_hi, pT_lo), 2 * P * r, 2 * P))
                mm.then_inc(w2_mm, 1)
                if left:
                    pe.wait_ge(es_made, n)
                    transposes(es[nxt], HG // 2).then_inc(esT_mm, 1)
                    running_sum(nxt, n, c == CB - 1)
                    pe.wait_ge(k_turned, n)
                    if last and c == CB - 1:
                        w_ready(g * 4 + 8)
                    project(WG, bank_kg, nxt).then_inc(g_mm, 1)
                    pe.wait_ge(k_summed, n)
                    pe.wait_ge(esT_lo_made, n)
                    transposes(k_rot[nxt]).then_inc(kT_mm, 1)
                if not left:
                    tick(1, 1)
                    tick(2, 2)
                pe.wait_ge(w2_masked, i)
                pe.wait_ge(part_made, i)
                for h in range(HG):
                    head = slice(P * h, P * h + P)
                    mm = pe.matmul(bank_o[:, head], masked[:, head], v[now][:, head], start=h == 0, stop=c == 0,
                                   skip_group_check=True)
                if c:
                    pe.wait_ge(s2_lo_made, carried(u, c - 1))
                    for r in range(HG // 2):
                        mm = product(bank_o[:, 2 * DV * r:2 * DV * r + 2 * DV],
                                     cols((pair_pT_hi, pair_pT_lo), P * r, P), cols((s2_hi, s2_lo), 2 * DV * r, 2 * DV),
                                     start=False, skip_group_check=True)
                mm.then_inc(o_mm, 1)
                if c < CB - 1:
                    pe.wait_ge(enz_made, n)
                    for h in range(HG):
                        mm = pe.matmul(s1_acc[:, M * h:M * h + M], k_rot[now][:, P * h:P * h + P],
                                       es[now][:, M * h:M * h + M], start=False, stop=True, skip_group_check=True)
                    mm.then_inc(s1_mm, 1)
                    pe.wait_ge(v_lo_made, i)
                    for r in range(HG // 2):
                        mm = product(bank_s2[:, 2 * DV * r:2 * DV * r + 2 * DV],
                                     cols((es_hi[now], es_lo[now]), P * r, P),
                                     cols((v_hi[now], v_lo[now]), 2 * DV * r, 2 * DV),
                                     start=c == 0 and r == 0, skip_group_check=True)
                    mm.then_inc(s2_mm, 1)
                if left:
                    scores(n)

            def ws2_cols(g, next_group):
                g = g + 1 if next_group else g
                return ws2_part[:, bass.ds(g * H, H)]

            all_steps(pe, step)
            tick(3, 3)
            pe.wait_ge(o_norm_made, STEPS + 1)
            transposes(o_gated).then_inc(oT_mm, 1)

            def last_out():
                pe.wait_ge(oT_lo_made, STEPS + 1)
                for h in range(HG):
                    mm = product(bank_o[:, :], cols((oT_hi, oT_lo), P * h, P), cols((wo_hi, wo_lo), D * h, D),
                                 start=h == 0, stop=h == HG - 1)
                mm.then_inc(out_mm, 1)

            last_out()
            last_phase(pe, 2, tick)


def kernel(**inputs):
    import numpy as np
    import concourse.bacc as bacc
    from concourse.bass_utils import run_bass_kernel_spmd

    def arr(name):
        return np.ascontiguousarray(inputs[name])

    hs = arr("L0_attn_hidden_states").reshape(CHUNKS, P, D)
    hs_cols = hs.reshape(CHUNKS, P, KT, P).transpose(0, 3, 2, 1).reshape(CHUNKS, P, KT * P)

    def grouped(w):
        return w.reshape(GROUPS, F, KT, P).transpose(0, 3, 2, 1).reshape(GROUPS, P, KT * F)

    wo = arr("L0_attn_Wo").reshape(D, GROUPS, HG, DV).transpose(1, 3, 2, 0).reshape(GROUPS, P, HG * D)
    w_groups = np.stack([grouped(arr("L0_attn_" + n)) for n in ("Wq", "Wk", "Wv", "Wg")] + [wo], axis=1)
    ws1 = np.zeros((P, KT, 4, 32), np.float32)
    ws1[:, :, :, :RANK] = arr("L0_attn_Ws1").reshape(RANK, KT, P).transpose(2, 1, 0)[:, :, None, :]
    ws2 = np.zeros((4, 32, HEADS * M), np.float32)
    ws2[:, :RANK] = arr("L0_attn_Ws2").T
    ws2[0::2, RANK] = arr("L0_attn_bs2")
    pos = np.arange(T, dtype=np.float32)
    inv_freq = (np.float32(1.0) / np.float32(10000.0) ** (np.arange(0, DK, 2, dtype=np.float32) / np.float32(DK)))
    ang = (pos[:, None] * inv_freq[None, :].astype(np.float32)).astype(np.float32)
    cos, sin = np.cos(ang).astype(np.float32), np.sin(ang).astype(np.float32)
    rope_cos = cos.reshape(CB, P, 64).transpose(1, 0, 2).reshape(P, CB * 64)
    rope_sin = np.concatenate([-sin, sin], axis=1).reshape(CB, P, 128).transpose(1, 0, 2).reshape(P, CB * 128)
    at = np.arange(P)
    keep_mask = (at[:, None] <= at[None, :]).astype(np.float32)
    small = {
        "cos": rope_cos,
        "sin": rope_sin,
        "keep": keep_mask,
        "below": 1 - keep_mask,
        "identity": np.eye(P, dtype=np.float32),
        "gnorm": arr("L0_attn_g_norm_weight").reshape(P, 1),
        "ws2": ws2.reshape(P, HEADS * M),
    }
    arrays = {
        "hs_cols": hs_cols,
        "hs_rows": hs,
        "w_groups": w_groups,
        "ws1": ws1.reshape(P, KT * P),
        "small": np.concatenate([small[name] for name in SMALL], axis=1),
        "ffn_w": arr("L0_ffn_weight").reshape(D, KT, P).transpose(2, 1, 0).reshape(P, KT * D),
        "ffn_scale": arr("L0_ffn_scale_weight"),
        "ffn_bias": arr("L0_ffn_bias"),
    }
    arrays = {n: np.ascontiguousarray(a) for n, a in arrays.items()}
    nc = bacc.Bacc("TRN2", target_bir_lowering=False, num_devices=1)
    args = [nc.dram_tensor(n, a.shape, mybir.dt.from_np(a.dtype), kind="ExternalInput").ap() for n, a in arrays.items()]
    out = nc.dram_tensor("out", (CHUNKS, P, D), F32, kind="ExternalOutput").ap()
    gated_slot_attention_block(nc, *args, out)
    result = run_bass_kernel_spmd(nc, [arrays], core_ids=[0])
    return result.results[0]["out"].reshape(BATCH, T, D)
```
